# Optimizing a Trainium2 kernel written in Bass

```python
import numpy as np
import jax
import jax.numpy as jnp

def _softmax(x, axis=-1):
    return jax.nn.softmax(x, axis=axis)

def _gelu(x):
    return jax.nn.gelu(x, approximate=True)

def _silu(x):
    return jax.nn.silu(x)

def _sigmoid(x):
    return jax.nn.sigmoid(x)

def _layernorm(x, axis=-1, eps=1e-05):
    m = jnp.mean(x, axis=axis, keepdims=True)
    v = jnp.var(x, axis=axis, keepdims=True)
    return (x - m) / jnp.sqrt(v + eps)

def _scatter_add(tgt, idx, src, axis=0):
    return tgt.at[idx].add(src)

def _segment_sum(src, seg, n):
    return jax.ops.segment_sum(src, seg, n)
kernel_name = 'mk_adj_preln_d1_adj_r2_a1c786'

def setup_inputs(seed: int=0):
    np.random.seed(seed)
    _w = jnp.asarray

    def _rec_inputs():
        import jax
        import jax.numpy as jnp
        _gk = jax.random.key(seed)
        x = -0.0005207 + 1.001 * jax.random.normal(jax.random.fold_in(_gk, 1), (8, 1024, 64), jnp.float32)
        _a = jax.random.bernoulli(jax.random.fold_in(_gk, 2), 0.0078125, (8, 1024, 1024))
        adj = _a.astype(jnp.int32)
        return (x, adj)
    x, adj = _rec_inputs()

    def _L0_gnn_setup():
        import jax, jax.numpy as jnp
        import numpy as np
        B, M, D, H, NBT = (128, 128, 64, 8, 5)
        NEG_SLOPE = 0.2
        key = jax.random.key(seed)
        ks = jax.random.split(key, 10)
        s = 1.0 / np.sqrt(D)
        sp = 1.0 / np.sqrt(D * H)
        return {'atom_embeddings': jax.random.normal(ks[0], (B, M, D), dtype=jnp.float32), 'edges': jax.random.randint(ks[1], (B, M, M), 0, NBT, dtype=jnp.int32), 'Wq': jax.random.normal(ks[2], (D, D * H), dtype=jnp.float32) * s, 'bq': jnp.zeros((D * H,), dtype=jnp.float32), 'Wk': jax.random.normal(ks[3], (D, D * H), dtype=jnp.float32) * s, 'bk': jnp.zeros((D * H,), dtype=jnp.float32), 'Wv': jax.random.normal(ks[4], (D, D * H), dtype=jnp.float32) * s, 'bv': jnp.zeros((D * H,), dtype=jnp.float32), 'edge_bias': jax.random.normal(ks[5], (NBT, H), dtype=jnp.float32) * 0.1, 'Wp': jax.random.normal(ks[6], (D * H, D), dtype=jnp.float32) * sp, 'bp': jnp.zeros((D,), dtype=jnp.float32)}
    _L0_gnn_all = _L0_gnn_setup()
    _L0_gnn_in = {k: v for k, v in _L0_gnn_all.items() if k in ('Wq', 'bq', 'Wk', 'bk', 'Wv', 'bv', 'edge_bias', 'Wp', 'bp')}
    del _L0_gnn_all
    return {'x': x, 'adj': adj, 'L0_gnn_Wq': _L0_gnn_in['Wq'], 'L0_gnn_bq': _L0_gnn_in['bq'], 'L0_gnn_Wk': _L0_gnn_in['Wk'], 'L0_gnn_bk': _L0_gnn_in['bk'], 'L0_gnn_Wv': _L0_gnn_in['Wv'], 'L0_gnn_bv': _L0_gnn_in['bv'], 'L0_gnn_edge_bias': _L0_gnn_in['edge_bias'], 'L0_gnn_Wp': _L0_gnn_in['Wp'], 'L0_gnn_bp': _L0_gnn_in['bp']}

def reference(x, adj, L0_gnn_Wq, L0_gnn_bq, L0_gnn_Wk, L0_gnn_bk, L0_gnn_Wv, L0_gnn_bv, L0_gnn_edge_bias, L0_gnn_Wp, L0_gnn_bp):
    import jax
    import jax.numpy as jnp

    def _L0_gnn_ref(atom_embeddings, edges, Wq, bq, Wk, bk, Wv, bv, edge_bias, Wp, bp):
        import jax, jax.numpy as jnp
        import numpy as np
        B, M, D, H, NBT = (128, 128, 64, 8, 5)
        NEG_SLOPE = 0.2
        b, m, d = atom_embeddings.shape
        h = edge_bias.shape[1]
        q = (atom_embeddings @ Wq + bq).reshape(b, m, h, d)
        k = (atom_embeddings @ Wk + bk).reshape(b, m, h, d)
        v = (atom_embeddings @ Wv + bv).reshape(b, m, h, d)
        scale = 1.0 / jnp.sqrt(jnp.asarray(d, dtype=q.dtype))
        scores = jnp.einsum('bmhd,bnhd->bhmn', q, k) * scale
        scores = scores + jnp.transpose(edge_bias[edges], (0, 3, 1, 2))
        scores = jax.nn.leaky_relu(scores, NEG_SLOPE)
        mask = (edges > 0)[:, None, :, :]
        scores = jnp.where(mask, scores, jnp.asarray(-1000000000.0, dtype=scores.dtype))
        attn = jax.nn.softmax(scores, axis=-1)
        out = jnp.einsum('bhmn,bnhd->bmhd', attn, v).reshape(b, m, h * d)
        return out @ Wp + bp
    h = jnp.maximum(_layernorm(x, axis=-1), 0.0)
    x = x + _L0_gnn_ref(h, adj, L0_gnn_Wq, L0_gnn_bq, L0_gnn_Wk, L0_gnn_bk, L0_gnn_Wv, L0_gnn_bv, L0_gnn_edge_bias, L0_gnn_Wp, L0_gnn_bp)
    return x

_drawn_inputs = setup_inputs


def setup_inputs(seed=0):
    import zlib

    import numpy as np

    out = dict(_drawn_inputs(seed))
    spreads = {'L0_gnn_bq': (0.0, 0.8),
     'L0_gnn_bk': (0.0, 0.8),
     'L0_gnn_bv': (0.0, 0.1),
     'L0_gnn_bp': (0.0, 0.1)}
    factors = {'L0_gnn_edge_bias': 6.929}
    for name, (base, spread) in spreads.items():
        noise = np.random.default_rng([zlib.crc32(name.encode()), seed]).standard_normal(out[name].shape)
        drawn = base * np.exp(spread * noise) if base else spread * noise
        out[name] = jnp.asarray(drawn.astype(out[name].dtype))
    for name, factor in factors.items():
        out[name] = (out[name] * factor).astype(out[name].dtype)
    return out
```

```python
from contextlib import ExitStack

import concourse.bass as bass
from concourse import mybir

ALU = mybir.AluOpType
ACT = mybir.ActivationFunctionType
AX_X = mybir.AxisListType.X
F32 = mybir.dt.float32
F32R = mybir.dt.float32r
BF16 = mybir.dt.bfloat16
I32 = mybir.dt.int32

P = 128
NEG = -(2.0 ** 100)
LEAST = -3.0e38
EPS = 1e-5


def preln_graph_attention(nc, x, adj, Wq, bq, Wk, bk, Wv, bv, edge_bias, Wp, bp, out):
    B, M, D = x.shape
    H = edge_bias.shape[1]
    assert (D, H, M % (8 * P)) == (64, 8, 0) and M == 1024
    TILES = B * M // P
    TPG = M // P
    MT = TPG // 2
    BLK = MT * P
    PAIRS = H // 2
    GPB = 2 * H
    LAG = 3
    QSCALE = 1.0 / 8.0

    x_tiles = x.rearrange("b (t p) d -> p (b t) d", p=P)
    x_blocks = x.rearrange("b (k t p) d -> (b k) p t d", p=P, t=MT)
    out_blocks = out.rearrange("b (k t p) d -> (b k) p t d", p=P, t=MT)
    adj_tiles = adj.rearrange("b (t p) n -> (b t) p n", p=P)

    with ExitStack() as ctx:
        def sb(name, shape, dt=F32):
            return ctx.enter_context(nc.sbuf_tensor(name, shape, dt))

        def sem(name):
            return ctx.enter_context(nc.semaphore(name))

        h_twice_hi = sb("h_twice_hi", [P, B * M], F32R)
        h_twice_lo = sb("h_twice_lo", [P, B * M], F32R)
        h_rows = sb("h_rows", [P, TILES, D])
        v_ones = sb("v_ones", [P, TPG, D + 1])
        beta = sb("beta", [P, 4 * TILES * 2])
        beta_quarter = sb("beta_quarter", [P, 4 * TILES * 2])
        g_parts = sb("g_parts", [P, H * D], F32R)
        q_bias = sb("q_bias", [P, PAIRS])
        vp = sb("vp", [P, PAIRS, D])
        out_const = sb("out_const", [P, D])
        ident = sb("ident", [P, P])
        w = sb("w", [P, 8, M])
        r = sb("r", [P, 2, M])
        pt = sb("pt", [P, 2, TPG, BLK])
        masks = sb("masks", [P, TPG, M], BF16)
        adj_in = sb("adj_in", [P, 2, M], I32)
        qt = sb("qt", [P, 2, BLK], F32R)
        o_copy = sb("o_copy", [D + 1, BLK])
        o_norm = sb("o_norm", [P, MT, 2, D])
        o_turned = sb("o_turned", [P, PAIRS, BLK])
        x_res = sb("x_res", [P, 2, MT, D])
        out_rows = sb("out_rows", [P, 2, MT, D])
        wmax = sb("wmax", [P, 2, MT])
        vmax = sb("vmax", [P, MT])
        vmax_leaky = sb("vmax_leaky", [P, MT])
        shift = sb("shift", [P, MT])
        den_inv = sb("den_inv", [P, MT])

        x_all = w[:, 0:4, :].rearrange("p s (t d) -> p (s t) d", d=D)
        x_sq = w[:, 4:8, :].rearrange("p s (t d) -> p (s t) d", d=D)
        temp = pt[:, :, :, :].rearrange("p s t m -> p (s t m)")
        wq_in, wk_in, wv_in = (temp[0:D, 512 * i:512 * i + 512] for i in range(3))
        wp_in = temp[:, 1536:1792].rearrange("p (c d) -> p c d", c=PAIRS)
        wqT, wkT, wvT = (temp[:, 2048 + 256 * i:2304 + 256 * i].rearrange("p (c d) -> p c d", c=PAIRS)
                         for i in range(3))
        bq_col, bk_col, bv_col, bqk = (temp[:, 2816 + 4 * i:2820 + 4 * i] for i in range(4))
        bp_row = temp[0:1, 2832:2896]
        eb_row = temp[0:1, 2896:2904].rearrange("p (c a) -> p a c", a=2)
        ones = temp[:, 2944:3072]
        wp_bv = temp[:, 3072:3328].rearrange("p (c d) -> p c d", c=PAIRS)
        head_const = temp[:, 3328:3336]
        h_doubled = temp[:, 4096:6144].rearrange("p (s t a d) -> p s t a d", s=4, t=MT, a=2)
        row_sum = temp[:, 3392:3456]
        row_var = temp[:, 3456:3520]
        row_std = temp[:, 3520:3584]
        row_rstd = temp[:, 3584:3648]
        u_parts = sb("u_parts", [P, H], F32R)

        bank = [ctx.enter_context(nc.psum_tensor(f"bank{i}", [P, 1024 if i < 2 else 512], F32)) for i in range(6)]
        score_banks = bank[0:2]
        turn_banks = bank[2:4]
        o_bank = bank[4]
        misc = bank[5]

        weights_in = sem("weights_in")
        x_in = [sem(f"x_in{i}") for i in range(2)]
        ident_zero = sem("ident_zero")
        ident_ready = sem("ident_ready")
        ones_ready = sem("ones_ready")
        ln_step = sem("ln_step")
        squares_ready = sem("squares_ready")
        std_ready = sem("std_ready")
        h_ready = sem("h_ready")
        w_turned = sem("w_turned")
        wT_ready = sem("wT_ready")
        bias_products = sem("bias_products")
        fold_ready = sem("fold_ready")
        hi_weights = sem("hi_weights")
        folded = sem("folded")
        h_doubled_ready = sem("h_doubled_ready")
        h_turned = sem("h_turned")
        h_hi = sem("h_hi")
        h_lo = sem("h_lo")
        beta_products = sem("beta_products")
        beta_ready = sem("beta_ready")
        adj_landed = [sem(f"adj_landed{i}") for i in range(2)]
        clamped = sem("clamped")
        masks_ready = sem("masks_ready")
        v_copied = sem("v_copied")
        q_products = sem("q_products")
        q_hi = sem("q_hi")
        q_lo = sem("q_lo")
        scores_ready = sem("scores_ready")
        scores_taken = sem("scores_taken")
        vmax_ready = sem("vmax_ready")
        leaky_ready = sem("leaky_ready")
        shift_ready = sem("shift_ready")
        relu_ready = sem("relu_ready")
        y_ready = sem("y_ready")
        y_turned = sem("y_turned")
        probs_ready = sem("probs_ready")
        pv_done = sem("pv_done")
        o_copied = sem("o_copied")
        o_rows = sem("o_rows")
        den_ready = sem("den_ready")
        o_normed = sem("o_normed")
        pair_turned = sem("pair_turned")
        pair_copied = sem("pair_copied")
        out_products = sem("out_products")
        res_ready = sem("res_ready")
        out_ready = sem("out_ready")
        x_res_in = [sem(f"x_res_in{i}") for i in range(2)]
        out_done = [sem(f"out_done{i}") for i in range(2)]

        def graph_of(b, g):
            return (b, g) if g < GPB else ((b + 1) % B, g - GPB)

        block = ctx.enter_context(nc.Block())

        @block.sync
        def _(sp):
            for i in range(2):
                sp.dma_start(x_all[:, 32 * i:32 * i + 32, :], x_tiles[:, 32 * i:32 * i + 32, :]).then_inc(x_in[i], 16)
            for dst, src in ((wq_in, Wq), (wk_in, Wk), (wv_in, Wv),
                             (wp_in, Wp.rearrange("(c p) d -> p c d", p=P))):
                sp.dma_start(dst, src).then_inc(weights_in, 16)
            for dst, src in ((bq_col, bq), (bk_col, bk), (bv_col, bv)):
                with nc.allow_non_contiguous_dma(reason="three vectors of 512"):
                    sp.dma_start(dst, src.rearrange("(c p) -> p c", p=P)).then_inc(weights_in, 16)
            sp.dma_start(bp_row, bp.rearrange("(a d) -> a d", a=1)).then_inc(weights_in, 16)
            sp.dma_start(temp[0:1, 2896:2904], edge_bias[1:2, :]).then_inc(weights_in, 16)
            for half in range(2):
                sp.dma_start(x_res[:, half], x_blocks[half]).then_inc(x_res_in[half], 16)

            def load_adj(b, src_b, t):
                k = TPG * b + t
                if not isinstance(k, int) or k >= 2:
                    sp.wait_ge(masks_ready, k - 1)
                sp.dma_start(adj_in[:, t % 2, :], adj_tiles[bass.ds(TPG * src_b + t, 1)].rearrange("a p n -> (a p) n"))\
                    .then_inc(adj_landed[t % 2], 16)

            for t in range(TPG):
                load_adj(0, 0, t)
            with sp.Fori(0, B) as b:
                nxt = (b + 1) % B
                for half in range(2):
                    for t in range(MT * half, MT * half + MT):
                        load_adj(b + 1, nxt, t)
                    sp.wait_ge(out_ready, 2 * b + half + 1)
                    sp.dma_start(out_blocks[bass.ds(2 * b + half, 1)].rearrange("a p t d -> p (a t) d"),
                                 out_rows[:, half]).then_inc(out_done[half], 16)
                    sp.wait_ge(out_done[half], 16 * b + 16)
                    sp.dma_start(x_res[:, half], x_blocks[bass.ds(2 * nxt + half, 1)]
                                 .rearrange("a p t d -> p (a t) d")).then_inc(x_res_in[half], 16)
            for half in range(2):
                sp.wait_ge(x_res_in[half], 16 * (B + 1))

        @block.gpsimd
        def _(pool):
            nc.gpsimd.memset(ident[:, :], 0.0).then_inc(ident_zero, 1)
            pool.wait_ge(ident_zero, 1)
            nc.gpsimd.affine_select(out=ident[:, :], in_=ident[:, :], compare_op=ALU.not_equal, fill=1.0, base=0,
                                    pattern=[[-1, P]], channel_multiplier=1).then_inc(ident_ready, 1)
            nc.gpsimd.memset(ones, 1.0).then_inc(ones_ready, 1)
            nc.gpsimd.memset(v_ones[:, :, D:D + 1], 1.0).then_inc(ones_ready, 1)

            def make_mask(b, t):
                k = TPG * b + t
                pool.wait_ge(adj_landed[t % 2], 16 * (MT * b + t // 2 + 1))
                pool.nop(nofuse=True)
                nc.gpsimd.tensor_scalar(masks[:, t, :], adj_in[:, t % 2, :], 1.0, 0.0, ALU.min, ALU.max)\
                    .then_inc(clamped, 1)
                pool.wait_ge(clamped, k + 1)
                pool.nop(nofuse=True)
                nc.gpsimd.tensor_scalar(masks[:, t, :], masks[:, t, :], -1.0, -NEG, ALU.add, ALU.mult)\
                    .then_inc(masks_ready, 1)

            def copy_v(src_b):
                nc.gpsimd.tensor_copy(v_ones[:, :, 0:D], h_rows[:, bass.ds(TPG * src_b, TPG), :]).then_inc(v_copied, 1)

            for t in range(TPG):
                make_mask(0, t)
            for k in range(2 * B):
                pool.wait_ge(h_ready, k // B + 1)
                if k >= 4:
                    pool.wait_ge(h_turned, k - 3)
                for a in range(2):
                    nc.gpsimd.tensor_copy(h_doubled[:, k % 4, :, a, :], h_rows[:, MT * k:MT * k + MT, :])\
                        .then_inc(h_doubled_ready, 1)
            copy_v(0)
            with pool.Fori(0, B) as b:
                pool.wait_ge(scores_taken, 64 * b + 32)
                for t in range(MT):
                    make_mask(b + 1, t)
                pool.wait_ge(scores_taken, 64 * b + 64)
                for t in range(MT, TPG):
                    make_mask(b + 1, t)
                pool.wait_ge(pv_done, GPB * b + GPB)
                copy_v((b + 1) % B)

        @block.tensor
        def _(pe):
            pe.wait_ge(weights_in, 16 * 9)
            pe.wait_ge(ident_ready, 1)
            for src, dst, c0 in ((wq_in, turn_banks[0], 0), (wk_in, turn_banks[0], 256), (wv_in, turn_banks[1], 0)):
                for c in range(PAIRS):
                    last = pe.transpose(dst[:, c0 + D * c:c0 + D * c + D], src[:, P * c:P * c + P], ident[0:D, 0:D])
            last.then_inc(w_turned, 1)
            pe.wait_ge(wT_ready, 3)
            pe.wait_ge(ones_ready, 1)
            pe.wait_ge(bias_products, PAIRS + 1)
            for a in range(2):
                rows = slice(D * a, D * a + D)
                first, second = score_banks[a][:, 0:512], score_banks[a][:, 512:1024]
                for c in range(PAIRS):
                    pe.matmul(first[0:D, D * c:D * c + D], wqT[rows, c, :], wkT[rows, c, :], start=True, stop=True)
                    pe.matmul(first[0:D, 256 + c:257 + c], wqT[rows, c, :], bk_col[rows, c:c + 1], start=True, stop=True)
                    pe.matmul(second[rows, D * c:D * c + D], wvT[rows, c, :], wp_in[rows, c, :], start=True, stop=True)
                    pe.matmul(second[rows, 256 + c:257 + c], wkT[rows, c, :], bq_col[rows, c:c + 1],
                              start=True, stop=True)
                sums = (o_bank, misc)[a][:, 0:PAIRS]
                pe.matmul(sums, ones[rows, :], bqk[rows, :], start=True, stop=False)
                last = pe.matmul(sums, ones[0:1, :], eb_row[:, a, :], start=False, stop=True)
            last.then_inc(fold_ready, 1)
            pe.wait_ge(wT_ready, 3)
            for c in range(PAIRS):
                pe.matmul(turn_banks[0][:, 0:D], ones, wp_bv[:, c, :], start=(c == 0), stop=False)
            pe.matmul(turn_banks[0][:, 0:D], ones[0:1, :], bp_row, start=False, stop=True).then_inc(fold_ready, 1)
            pe.wait_ge(h_ready, 2)
            pe.wait_ge(folded, 6)

            def turn_h(k):
                if k >= 4:
                    pe.wait_ge(h_lo, k - 3)
                pe.wait_ge(h_doubled_ready, 2 * k + 2)
                dst = score_banks[k % 4 // 2][:, 512 * (k % 2):512 * (k % 2) + 512]
                for t in range(MT):
                    last = pe.transpose(dst[:, P * t:P * t + P],
                                        h_doubled[:, k % 4, t].rearrange("p a d -> p (a d)"), ident[:, :])
                last.then_inc(h_turned, 1)

            def beta_block(k):
                pe.wait_ge(h_lo, k + 1)
                for t in range(MT * k, MT * k + MT):
                    dst = turn_banks[1][:, H * t:H * t + H]
                    pe.matmul(dst, h_twice_hi[:, P * t:P * t + P], u_parts[:, :], start=True, stop=False)
                    last = pe.matmul(dst, h_twice_lo[:, P * t:P * t + P], u_parts[:, :], start=False, stop=True)
                last.then_inc(beta_products, 1)

            for k in range(2 * B + 2):
                if k < 2 * B:
                    turn_h(k)
                if k >= 2:
                    beta_block(k - 2)
            pe.wait_ge(beta_ready, 2 * B + 1)

            def scores(b, g, mt):
                u = 4 * (GPB * b + g) + mt
                gb, gg = graph_of(b, g)
                pe.wait_ge(q_lo, GPB * b + g + 1)
                if not isinstance(u, int) or u >= 2:
                    pe.wait_ge(scores_taken, u - 1)
                for j in range(2):
                    dst = score_banks[mt % 2][:, 512 * j:512 * j + 512]
                    stat = qt[:, g % 2, P * mt:P * mt + P]
                    pe.matmul(dst, stat, h_twice_hi[:, bass.ds(M * gb + 512 * j, 512)], start=True, stop=False)
                    last = pe.matmul(dst, stat, h_twice_lo[:, bass.ds(M * gb + 512 * j, 512)], start=False, stop=True)
                last.then_inc(scores_ready, 1)

            def project_q(b, g):
                gb, gg = graph_of(b, g)
                half, c = gg // H, gg % H // 2
                for n, part in enumerate((h_twice_hi, h_twice_lo)):
                    last = pe.matmul(misc[:, :], g_parts[:, P * c:P * c + P],
                                     part[:, bass.ds(M * gb + BLK * half, BLK)], start=(n == 0), stop=(n == 1))
                last.then_inc(q_products, 1)

            def step(b, g, mt):
                n = GPB * b + g
                scores(b, g + (mt == MT - 1), (mt + 1) % MT)
                if g >= 1:
                    u = 4 * (n - 1) + mt
                    pe.wait_ge(y_ready, u + 1)
                    for j in range(2):
                        if not isinstance(u, int) or u >= 1:
                            pe.wait_ge(probs_ready, 2 * (u - 1) + j + 1)
                        for t in range(MT):
                            last = pe.transpose(turn_banks[j][:, P * t:P * t + P],
                                                w[:, 4 * ((g - 1) % 2) + mt, P * (MT * j + t):P * (MT * j + t) + P],
                                                ident[:, :])
                        last.then_inc(y_turned, 1)
                if g >= 2 and mt >= 1:
                    if mt == 1:
                        pe.wait_ge(probs_ready, 8 * (n - 2) + 8)
                        if not isinstance(n, int) or n >= 3:
                            pe.wait_ge(o_copied, n - 2)
                        if g % GPB == 2:
                            pe.wait_ge(v_copied, b + (g == GPB + 2) + 1)
                    for t in ((0, 1), (2, 3, 4), (5, 6, 7))[mt - 1]:
                        last = pe.matmul(o_bank[0:D + 1, :], v_ones[:, t, :], pt[:, g % 2, t, :],
                                         start=(t == 0), stop=(t == TPG - 1))
                    if mt == MT - 1:
                        last.then_inc(pv_done, 1)
                if g >= LAG and mt == 0:
                    pe.wait_ge(o_copied, n - 2)
                    pe.wait_ge(q_lo, n + 1 if g % 2 else n + 2)
                    for t in range(MT):
                        last = pe.transpose(misc[:, (D + 1) * t:(D + 1) * t + D + 1], o_copy[:, P * t:P * t + P],
                                            ident[0:D + 1, 0:D + 1])
                    last.then_inc(o_rows, 1)
                if g % 2 == 1 and mt == 1:
                    if g >= LAG:
                        pe.wait_ge(o_normed, n - 2)
                    project_q(b, g + 1)
                if g % 2 == 0 and g >= LAG and mt == 1:
                    pe.wait_ge(o_normed, n - 2)
                    for t in range(MT):
                        last = pe.transpose(misc[:, P * t:P * t + P], o_norm[:, t, :, :].rearrange("p a d -> p (a d)"),
                                            ident[:, :])
                    last.then_inc(pair_turned, 1)
                if g in (GPB // 2 + 2, GPB + 2) and mt == 2:
                    pe.wait_ge(pair_copied, H * b + (g - 2) // 2)
                    for t in range(MT):
                        for c in range(PAIRS):
                            last = pe.matmul(misc[:, D * t:D * t + D], o_turned[:, c, P * t:P * t + P], vp[:, c, :],
                                             start=(c == 0), stop=(c == PAIRS - 1))
                    last.then_inc(out_products, 1)

            project_q(0, 0)
            scores(0, 0, 0)
            for g in range(LAG):
                for mt in range(MT):
                    step(0, g, mt)
            with pe.Fori(0, B) as b:
                for g in range(LAG, LAG + GPB):
                    for mt in range(MT):
                        step(b, g, mt)

        @block.scalar
        def _(act):
            for i in range(2):
                t = slice(32 * i, 32 * i + 32)
                act.wait_ge(ln_step, 2 * i + 2)
                nc.scalar.activation(x_sq[:, t, :], x_all[:, t, :], ACT.Square).then_inc(squares_ready, 1)
            act.wait_ge(ln_step, 5)
            nc.scalar.activation(row_std, row_var, ACT.Sqrt).then_inc(std_ready, 1)
            act.wait_ge(fold_ready, 1)
            g_hi = g_parts[0:D, :].rearrange("p (c a d) -> p a c d", a=2, d=D)
            u_hi = u_parts[0:D, :].rearrange("p (c a) -> p a c", a=2)
            for a in range(2):
                nc.scalar.activation(g_hi[:, a], score_banks[a][0:D, 0:256].rearrange("p (c d) -> p c d", d=D),
                                     ACT.Copy, scale=QSCALE).then_inc(hi_weights, 1)
                nc.scalar.activation(u_hi[:, a], score_banks[a][0:D, 256:260], ACT.Copy, scale=QSCALE)\
                    .then_inc(hi_weights, 1)
            for k in range(2 * B):
                act.wait_ge(h_turned, k + 1)
                nc.scalar.activation(h_twice_hi[:, BLK * k:BLK * k + BLK],
                                     score_banks[k % 4 // 2][:, 512 * (k % 2):512 * (k % 2) + 512], ACT.Copy)\
                    .then_inc(h_hi, 1)

            def q_hi_part(b, g, a):
                n = GPB * b + g
                gb, gg = graph_of(b, g)
                c = gg % H // 2
                act.wait_ge(q_products, (GPB // 2) * b + g // 2 + 1)
                if not isinstance(n, int) or n >= 2:
                    act.wait_ge(scores_ready, 4 * (n - 2 + a) + 4)
                rows = slice(D * a, D * a + D)
                nc.scalar.activation(qt[0:D, a, :], misc[rows, :], ACT.Identity, bias=q_bias[rows, c:c + 1])\
                    .then_inc(q_hi, 1)

            def step(b, g, mt):
                n = GPB * b + g
                if g >= 1:
                    u = 4 * (n - 1) + mt
                    gb, gg = graph_of(b, g - 1)
                    if not isinstance(u, int) or u >= 2:
                        act.wait_ge(y_ready, u - 1)
                    act.wait_ge(scores_taken, u + 1)
                    nc.scalar.activation(r[:, mt % 2, :], w[:, 4 * ((g - 1) % 2) + mt, :], ACT.Relu,
                                         bias=beta[:, bass.ds(4 * (GPB * gb + gg) + mt, 1)], scale=4.0)\
                        .then_inc(relu_ready, 1)
                ge, me = (g - 1, mt - 1) if mt else (g - 2, MT - 1)
                if ge >= 0:
                    ne = GPB * b + ge
                    u = 4 * ne + me
                    if me == 0 and (not isinstance(ne, int) or ne >= 2):
                        act.wait_ge(pv_done, ne - 1)
                    for j in range(2):
                        act.wait_ge(y_turned, 2 * u + j + 1)
                        nc.scalar.activation(pt[:, ge % 2, MT * j:MT * j + MT, P * me:P * me + P],
                                             turn_banks[j][:, :].rearrange("p (t m) -> p t m", t=MT),
                                             ACT.Exp, scale=0.8).then_inc(probs_ready, 1)
                if g % 2 == 1 and mt in (1, 3):
                    q_hi_part(b, g + 1, mt // 2)
                if g >= LAG and mt == 0:
                    act.wait_ge(pv_done, n - 2)
                    if not isinstance(n, int) or n >= 4:
                        act.wait_ge(o_rows, n - 3)
                    nc.scalar.activation(o_copy[:, :], o_bank[0:D + 1, :], ACT.Copy).then_inc(o_copied, 1)
                if g % 2 == 0 and g >= LAG and mt == 1:
                    c = (g - 4) // 2 % PAIRS
                    act.wait_ge(pair_turned, (GPB // 2) * b + (g - 2) // 2)
                    nc.scalar.activation(o_turned[:, c, :], misc[:, :], ACT.Copy).then_inc(pair_copied, 1)

            for a in range(2):
                if a == 0:
                    act.wait_ge(folded, 6)
                q_hi_part(0, 0, a)
            for g in range(LAG):
                for mt in range(MT):
                    step(0, g, mt)
            with act.Fori(0, B) as b:
                for g in range(LAG, LAG + GPB):
                    for mt in range(MT):
                        step(b, g, mt)

        @block.vector
        def _(dve):
            for i in range(2):
                t = slice(32 * i, 32 * i + 32)
                dve.wait_ge(x_in[i], 16)
                nc.vector.tensor_reduce(row_sum[:, t], x_all[:, t, :], AX_X, ALU.add).then_inc(ln_step, 1)
                dve.wait_ge(ln_step, 2 * i + 1)
                nc.vector.scalar_tensor_tensor(x_all[:, t, :], row_sum[:, t].unsqueeze(2).to_broadcast([P, 32, D]),
                                               -1.0 / D, x_all[:, t, :], ALU.mult, ALU.add).then_inc(ln_step, 1)
            dve.wait_ge(squares_ready, 2)
            nc.vector.tensor_reduce(row_sum, x_sq, AX_X, ALU.add).then_inc(bias_products, 1)
            dve.wait_ge(weights_in, 16 * 9)
            dve.wait_ge(bias_products, 1)
            nc.vector.tensor_scalar(row_var, row_sum, 1.0 / D, EPS, ALU.mult, ALU.add).then_inc(ln_step, 1)
            nc.vector.scalar_tensor_tensor(bqk, bq_col, QSCALE, bk_col, ALU.mult, ALU.mult)
            for c in range(PAIRS):
                nc.vector.tensor_scalar(wp_bv[:, c, :], wp_in[:, c, :], bv_col[:, c:c + 1], None, ALU.mult)\
                    .then_inc(bias_products, 1)
            dve.wait_ge(w_turned, 1)
            for dst, src in ((wqT, turn_banks[0][:, 0:256]), (wkT, turn_banks[0][:, 256:512]),
                             (wvT, turn_banks[1][:, 0:256])):
                nc.vector.tensor_copy(dst, src.rearrange("p (c d) -> p c d", d=D)).then_inc(wT_ready, 1)
            dve.wait_ge(std_ready, 1)
            nc.vector.reciprocal(row_rstd, row_std).then_inc(ln_step, 1)
            dve.wait_ge(ln_step, 6)
            for i in range(2):
                t = slice(32 * i, 32 * i + 32)
                nc.vector.scalar_tensor_tensor(h_rows[:, t, :], x_all[:, t, :], 0.0,
                                               row_rstd[:, t].unsqueeze(2).to_broadcast([P, 32, D]),
                                               ALU.max, ALU.mult).then_inc(h_ready, 1)
            dve.wait_ge(fold_ready, 2)
            dve.wait_ge(hi_weights, 4)
            g_hi, g_lo = (g_parts[rows, :].rearrange("p (c a d) -> p a c d", a=2, d=D) for rows in
                          (slice(0, D), slice(D, P)))
            u_hi, u_lo = (u_parts[rows, :].rearrange("p (c a) -> p a c", a=2) for rows in (slice(0, D), slice(D, P)))
            for a in range(2):
                rows = slice(D * a, D * a + D)
                first, second = score_banks[a][:, 0:512], score_banks[a][:, 512:1024]
                nc.vector.scalar_tensor_tensor(g_lo[:, a], first[0:D, 0:256].rearrange("p (c d) -> p c d", d=D),
                                               QSCALE, g_hi[:, a].bitcast(F32), ALU.mult, ALU.subtract)
                nc.vector.scalar_tensor_tensor(u_lo[:, a], first[0:D, 256:260], QSCALE, u_hi[:, a].bitcast(F32),
                                               ALU.mult, ALU.subtract).then_inc(folded, 1)
                nc.vector.tensor_copy(vp[rows, :, :], second[rows, 0:256].rearrange("p (c d) -> p c d", d=D))
                nc.vector.tensor_scalar(q_bias[rows, :], second[rows, 256:260], QSCALE, None, ALU.mult)\
                    .then_inc(folded, 1)
                nc.vector.tensor_copy(head_const.rearrange("p (c a) -> p a c", a=2)[:, a],
                                      (o_bank, misc)[a][:, 0:PAIRS])
            nc.vector.tensor_copy(out_const[:, :], turn_banks[0][:, 0:D]).then_inc(folded, 2)
            for k in range(2 * B):
                dve.wait_ge(h_hi, k + 1)
                cols = slice(BLK * k, BLK * k + BLK)
                nc.vector.tensor_tensor(h_twice_lo[:, cols], score_banks[k % 4 // 2][:, 512 * (k % 2):512 * (k % 2) + 512],
                                        h_twice_hi[:, cols].bitcast(F32), ALU.subtract).then_inc(h_lo, 1)
            dve.wait_ge(beta_products, 2 * B)
            for k in range(2 * B):
                last = nc.vector.tensor_tensor(beta[:, 32 * k:32 * k + 32].rearrange("p (h t) -> p h t", h=H),
                                               turn_banks[1][:, 32 * k:32 * k + 32].rearrange("p (t h) -> p h t", h=H),
                                               head_const.unsqueeze(2).to_broadcast([P, H, MT]), ALU.add)
                last.then_inc(beta_ready, 1)
            dve.wait_ge(beta_ready, 2 * B)
            nc.vector.tensor_scalar(beta_quarter[:, :], beta[:, :], 0.25, None, ALU.mult).then_inc(beta_ready, 1)

            def q_lo_part(b, g, a):
                gb, gg = graph_of(b, g)
                c = gg % H // 2
                rows = slice(D * a, D * a + D)
                dve.wait_ge(q_hi, GPB * b + g + a + 1)
                nc.vector.scalar_tensor_tensor(qt[D:P, a, :], misc[rows, :], q_bias[rows, c:c + 1],
                                               qt[0:D, a, :].bitcast(F32), ALU.add, ALU.subtract).then_inc(q_lo, 1)

            def step(b, g, mt):
                n = GPB * b + g
                u = 4 * n + mt
                gb, gg = graph_of(b, g)
                half = gg // H
                if gg % H == 0:
                    dve.wait_ge(masks_ready, TPG * (b + g // GPB) + MT * half + mt + 1)
                if not isinstance(n, int) or n >= 2:
                    dve.wait_ge(y_turned, 2 * (u - 8) + 2)
                dve.wait_ge(scores_ready, u + 1)
                dve.nop(nofuse=True)
                nc.vector.tensor_tensor_reduce(w[:, 4 * (g % 2) + mt, :], score_banks[mt % 2][:, :],
                                               masks[:, MT * half + mt, :], 0.25, LEAST, ALU.add, ALU.max,
                                               wmax[:, g % 2, mt:mt + 1]).then_inc(scores_taken, 1)
                if g >= 1:
                    gb, gg = graph_of(b, g - 1)
                    if mt == 0:
                        cols = bass.ds(4 * (GPB * gb + gg), MT)
                        dve.wait_ge(scores_taken, 4 * n)
                        nc.vector.scalar_tensor_tensor(vmax[:, :], wmax[:, (g - 1) % 2, :], 4.0, beta[:, cols],
                                                       ALU.mult, ALU.add).then_inc(vmax_ready, 1)
                        dve.wait_ge(vmax_ready, n)
                        nc.vector.scalar_tensor_tensor(vmax_leaky[:, :], vmax[:, :], 5.0, vmax[:, :],
                                                       ALU.mult, ALU.max).then_inc(leaky_ready, 1)
                        dve.wait_ge(leaky_ready, n)
                        if not isinstance(n, int) or n >= 2:
                            dve.wait_ge(y_ready, 4 * (n - 1))
                        nc.vector.scalar_tensor_tensor(shift[:, :], vmax_leaky[:, :], -0.25, beta_quarter[:, cols],
                                                       ALU.mult, ALU.add).then_inc(shift_ready, 1)
                        dve.wait_ge(shift_ready, n)
                    dve.wait_ge(relu_ready, 4 * (n - 1) + mt + 1)
                    y = w[:, 4 * ((g - 1) % 2) + mt, :]
                    nc.vector.scalar_tensor_tensor(y, y, shift[:, mt:mt + 1], r[:, mt % 2, :], ALU.add, ALU.add)\
                        .then_inc(y_ready, 1)
                if g >= LAG and mt == 0:
                    rows = misc[:, 0:(D + 1) * MT].rearrange("p (t d) -> p t d", t=MT)
                    dve.wait_ge(o_rows, n - 2)
                    nc.vector.reciprocal(den_inv[:, :].unsqueeze(2), rows[:, :, D:D + 1]).then_inc(den_ready, 1)
                    dve.wait_ge(den_ready, n - 2)
                    nc.vector.tensor_tensor(o_norm[:, :, (g - LAG) % 2, :], rows[:, :, 0:D],
                                            den_inv[:, :].unsqueeze(2).to_broadcast([P, MT, D]), ALU.mult)\
                        .then_inc(o_normed, 1)
                if g % 2 == 1 and mt in (1, 3):
                    q_lo_part(b, g + 1, mt // 2)
                if g in (GPB // 2 + 2, GPB + 2) and mt == 3:
                    half = g // GPB
                    dve.wait_ge(x_res_in[half], 16 * b + 16)
                    nc.vector.tensor_tensor(x_res[:, half], x_res[:, half],
                                            out_const[:, :].unsqueeze(1).to_broadcast([P, MT, D]), ALU.add)\
                        .then_inc(res_ready, 1)
                    dve.wait_ge(res_ready, 2 * b + half + 1)
                    dve.wait_ge(out_products, 2 * b + half + 1)
                    nc.vector.tensor_tensor(out_rows[:, half], misc[:, 0:D * MT].rearrange("p (t d) -> p t d", t=MT),
                                            x_res[:, half], ALU.add).then_inc(out_ready, 1)

            for a in range(2):
                q_lo_part(0, 0, a)
            for g in range(LAG):
                for mt in range(MT):
                    step(0, g, mt)
            with dve.Fori(0, B) as b:
                for g in range(LAG, LAG + GPB):
                    for mt in range(MT):
                        step(b, g, mt)


_INS = ["x", "adj", "L0_gnn_Wq", "L0_gnn_bq", "L0_gnn_Wk", "L0_gnn_bk", "L0_gnn_Wv", "L0_gnn_bv",
        "L0_gnn_edge_bias", "L0_gnn_Wp", "L0_gnn_bp"]


def kernel(**inputs):
    import numpy as _np
    import concourse.bacc as _bacc
    from concourse import mybir as _mybir
    from concourse.bass_utils import run_bass_kernel_spmd as _run

    nc = _bacc.Bacc("TRN2", target_bir_lowering=False, num_devices=1)
    arrays, args = {}, []
    for name in _INS:
        a = _np.ascontiguousarray(inputs[name])
        arrays[f"in_{name}_dram"] = a
        args.append(nc.dram_tensor(f"in_{name}_dram", a.shape, _mybir.dt.from_np(a.dtype), kind="ExternalInput").ap())
    shape = tuple(inputs["x"].shape)
    out = nc.dram_tensor("out_0_dram", shape, _mybir.dt.float32, kind="ExternalOutput").ap()
    preln_graph_attention(nc, *args, out)
    r = _run(nc, [arrays], core_ids=[0])
    return r.results[0]["out_0_dram"]
```

```python
from contextlib import ExitStack

import concourse.bass as bass
from concourse import mybir

ALU = mybir.AluOpType
ACT = mybir.ActivationFunctionType
AX_X = mybir.AxisListType.X
F32 = mybir.dt.float32
F32R = mybir.dt.float32r
BF16 = mybir.dt.bfloat16
I32 = mybir.dt.int32

P = 128
NEG = -(2.0 ** 100)
LEAST = -3.0e38
EPS = 1e-5


def preln_graph_attention(nc, x, adj, Wq, bq, Wk, bk, Wv, bv, edge_bias, Wp, bp, out):
    B, M, D = x.shape
    H = edge_bias.shape[1]
    assert (D, H, M % (8 * P)) == (64, 8, 0) and M == 1024
    TILES = B * M // P
    TPG = M // P
    MT = TPG // 2
    BLK = MT * P
    PAIRS = H // 2
    UNITS = 2 * H * MT
    QSCALE = 1.0 / 8.0
    RELU, Y, TURN, EXP = 3, 4, 5, 6
    PV, O_COPY, DEN, DEN_INV, ROWS, NORM, PAIR, PROJECT, FINAL = 15, 22, 21, 22, 23, 24, 25, 26, 27
    QT = 5
    K0 = 20

    x_tiles = x.rearrange("b (t p) d -> p (b t) d", p=P)
    x_blocks = x.rearrange("b (k t p) d -> (b k) p t d", p=P, t=MT)
    out_blocks = out.rearrange("b (k t p) d -> (b k) p t d", p=P, t=MT)
    adj_tiles = adj.rearrange("b (t p) n -> (b t) p n", p=P)

    with ExitStack() as ctx:
        def sb(name, shape, dt=F32):
            return ctx.enter_context(nc.sbuf_tensor(name, shape, dt))

        def sem(name):
            return ctx.enter_context(nc.semaphore(name))

        h_twice_hi = sb("h_twice_hi", [P, 2 * M], F32R)
        h_twice_lo = sb("h_twice_lo", [P, 2 * M], F32R)
        v_next = sb("v_next", [P, TPG, D])
        v_now = sb("v_now", [P, TPG, D])
        ones_col = sb("ones_col", [P, 1])
        beta = sb("beta", [P, B * UNITS])
        g_parts = sb("g_parts", [P, H * D], F32R)
        q_bias = sb("q_bias", [P, PAIRS])
        vp = sb("vp", [P, PAIRS, D])
        out_const = sb("out_const", [P, D])
        ident = sb("ident", [P, P])
        w = sb("w", [P, 8, M])
        r = sb("r", [P, 2, M])
        pt = sb("pt", [P, 2, 2, TPG, BLK])
        sum4 = sb("sum4", [P, TPG // 2, BLK])
        sum2 = sb("sum2", [P, TPG // 4, BLK])
        sum1 = sb("sum1", [P, 2, BLK])
        masks = sb("masks", [P, TPG, M], BF16)
        adj_in = sb("adj_in", [P, 2, M], I32)
        qt = sb("qt", [P, 2, 2, BLK], F32R)
        o_copy = sb("o_copy", [P, BLK])
        o_norm = sb("o_norm", [P, MT, 2 * D])
        o_turned = sb("o_turned", [P, PAIRS, BLK])
        x_res = sb("x_res", [P, 2, MT, D])
        out_rows = sb("out_rows", [P, 2, MT, D])
        wmax = sb("wmax", [P, 2, MT])
        shift_neg = sb("shift_neg", [P, MT])
        shift = sb("shift", [P, 2, MT])
        den_inv = sb("den_inv", [P, MT * 2])

        h_store = nc.dram_tensor("h_store", (P, TILES, D), F32, kind="Internal").ap()
        hi_store = nc.dram_tensor("hi_store", (P, B * M), F32, kind="Internal").ap()
        lo_store = nc.dram_tensor("lo_store", (P, B * M), F32, kind="Internal").ap()

        x_all = w[:, 0:4, :].rearrange("p s (t d) -> p (s t) d", d=D)
        x_sq = w[:, 4:8, :].rearrange("p s (t d) -> p (s t) d", d=D)
        temp = pt[:, :, :, :, :].rearrange("p s a t m -> p (s a t m)")
        h_rows = temp[:, 8192:12288].rearrange("p (t d) -> p t d", d=D)
        wq_in, wk_in, wv_in = (temp[0:D, 512 * i:512 * i + 512] for i in range(3))
        wp_in = temp[:, 1536:1792].rearrange("p (c d) -> p c d", c=PAIRS)
        wqT, wkT, wvT = (temp[:, 2048 + 256 * i:2304 + 256 * i].rearrange("p (c d) -> p c d", c=PAIRS)
                         for i in range(3))
        bq_col, bk_col, bv_col, bqk = (temp[:, 2816 + 4 * i:2820 + 4 * i] for i in range(4))
        bp_row = temp[0:1, 2832:2896]
        eb_row = temp[0:1, 2896:2904].rearrange("p (c a) -> p a c", a=2)
        ones = temp[:, 2944:3072]
        wp_bv = temp[:, 3072:3328].rearrange("p (c d) -> p c d", c=PAIRS)
        head_const = temp[:, 3328:3336]
        h_doubled = temp[:, 4096:6144].rearrange("p (s t a d) -> p s t a d", s=4, t=MT, a=2)
        row_sum = temp[:, 3392:3456]
        row_var = temp[:, 3456:3520]
        row_std = temp[:, 3520:3584]
        row_rstd = temp[:, 3584:3648]
        u_parts = sb("u_parts", [P, H], F32R)

        bank = [ctx.enter_context(nc.psum_tensor(f"bank{i}", [P, 1024 if i < 2 else 512], F32)) for i in range(6)]
        score_banks = bank[0:2]
        turn_banks = bank[2:4]
        o_bank = bank[4]
        misc = bank[5]

        weights_in = sem("weights_in")
        x_in = [sem(f"x_in{i}") for i in range(2)]
        ident_zero = sem("ident_zero")
        ident_ready = sem("ident_ready")
        ones_ready = sem("ones_ready")
        ln_step = sem("ln_step")
        squares_ready = sem("squares_ready")
        std_ready = sem("std_ready")
        h_ready = sem("h_ready")
        w_turned = sem("w_turned")
        wT_ready = sem("wT_ready")
        bias_products = sem("bias_products")
        fold_ready = sem("fold_ready")
        hi_weights = sem("hi_weights")
        folded = sem("folded")
        h_doubled_ready = sem("h_doubled_ready")
        h_turned = sem("h_turned")
        h_hi = sem("h_hi")
        h_lo = sem("h_lo")
        beta_products = sem("beta_products")
        beta_ready = sem("beta_ready")
        h_stored = sem("h_stored")
        parts_stored = [sem(f"parts_stored{i}") for i in range(4)]
        parts_in = sem("parts_in")
        v_in = sem("v_in")
        adj_landed = [sem(f"adj_landed{i}") for i in range(2)]
        clamped = sem("clamped")
        masks_ready = sem("masks_ready")
        v_copied = sem("v_copied")
        q_products = sem("q_products")
        q_hi = sem("q_hi")
        q_lo = sem("q_lo")
        scores_ready = sem("scores_ready")
        scores_taken = sem("scores_taken")
        neg_ready = sem("neg_ready")
        shift_ready = sem("shift_ready")
        relu_ready = sem("relu_ready")
        y_ready = sem("y_ready")
        y_turned = sem("y_turned")
        probs_ready = sem("probs_ready")
        pair_sums = sem("pair_sums")
        key_sums = sem("key_sums")
        pv_done = sem("pv_done")
        o_copied = sem("o_copied")
        den_products = sem("den_products")
        den_ready = sem("den_ready")
        o_rows = sem("o_rows")
        o_normed = sem("o_normed")
        pair_turned = sem("pair_turned")
        pair_copied = sem("pair_copied")
        out_products = sem("out_products")
        res_ready = sem("res_ready")
        out_ready = sem("out_ready")
        x_res_in = [sem(f"x_res_in{i}") for i in range(2)]
        out_done = [sem(f"out_done{i}") for i in range(2)]

        def graph_of(b, k):
            return (b, k) if k < UNITS else ((b + 1) % B, k - UNITS)

        def later(count, least=1):
            return not isinstance(count, int) or count >= least

        block = ctx.enter_context(nc.Block())

        @block.sync
        def _(sp):
            for i in range(2):
                sp.dma_start(x_all[:, 32 * i:32 * i + 32, :], x_tiles[:, 32 * i:32 * i + 32, :]).then_inc(x_in[i], 16)
            for dst, src in ((wq_in, Wq), (wk_in, Wk), (wv_in, Wv),
                             (wp_in, Wp.rearrange("(c p) d -> p c d", p=P))):
                sp.dma_start(dst, src).then_inc(weights_in, 16)
            for dst, src in ((bq_col, bq), (bk_col, bk), (bv_col, bv)):
                with nc.allow_non_contiguous_dma(reason="three vectors of 512"):
                    sp.dma_start(dst, src.rearrange("(c p) -> p c", p=P)).then_inc(weights_in, 16)
            sp.dma_start(bp_row, bp.rearrange("(a d) -> a d", a=1)).then_inc(weights_in, 16)
            sp.dma_start(temp[0:1, 2896:2904], edge_bias[1:2, :]).then_inc(weights_in, 16)
            for half in range(2):
                sp.dma_start(x_res[:, half], x_blocks[half]).then_inc(x_res_in[half], 16)

            def load_adj(b, src_b, t):
                i = TPG * b + t
                if later(i, 2):
                    sp.wait_ge(masks_ready, i - 1)
                sp.dma_start(adj_in[:, t % 2, :], adj_tiles[bass.ds(TPG * src_b + t, 1)].rearrange("a p n -> (a p) n"))\
                    .then_inc(adj_landed[t % 2], 16)

            def load_parts(slot, src_b):
                for dst, src in ((h_twice_hi, hi_store), (h_twice_lo, lo_store)):
                    sp.dma_start(dst[:, bass.ds(M * slot, M)].bitcast(F32), src[:, bass.ds(M * src_b, M)]).then_inc(parts_in, 16)

            def load_v(src_b):
                sp.dma_start(v_next[:, :, :], h_store[:, bass.ds(TPG * src_b, TPG), :]).then_inc(v_in, 16)

            for t in range(2):
                load_adj(0, 0, t)
            sp.wait_ge(h_ready, 2)
            sp.dma_start(h_store, h_rows).then_inc(h_stored, 16)
            for k in range(2 * B):
                sp.wait_ge(h_lo, k + 1)
                sp.dma_start(hi_store[:, BLK * k:BLK * k + BLK], h_twice_hi[:, BLK * (k % 4):BLK * (k % 4) + BLK].bitcast(F32))\
                    .then_inc(parts_stored[k % 4], 16)
                sp.dma_start(lo_store[:, BLK * k:BLK * k + BLK], h_twice_lo[:, BLK * (k % 4):BLK * (k % 4) + BLK].bitcast(F32))\
                    .then_inc(parts_stored[k % 4], 16)
            sp.wait_ge(h_stored, 16)
            load_v(0)
            for i in range(4):
                sp.wait_ge(parts_stored[i], 32 * 2 * B // 4)
            sp.wait_ge(beta_products, 2 * B)
            load_parts(0, 0)
            for t in range(2, TPG):
                load_adj(0, 0, t)
            with sp.Fori(0, B) as b:
                nxt = (b + 1) % B
                for half in range(2):
                    load_adj(b + 1, nxt, MT * half)
                    load_adj(b + 1, nxt, MT * half + 1)
                    if half == 0:
                        sp.wait_ge(scores_ready, UNITS * b + 1)
                        load_parts(nxt % 2, nxt)
                        sp.wait_ge(v_copied, b + 1)
                        load_v(nxt)
                    load_adj(b + 1, nxt, MT * half + 2)
                    load_adj(b + 1, nxt, MT * half + 3)
                    sp.wait_ge(out_ready, 2 * b + half + 1)
                    sp.dma_start(out_blocks[bass.ds(2 * b + half, 1)].rearrange("a p t d -> p (a t) d"),
                                 out_rows[:, half]).then_inc(out_done[half], 16)
                    sp.wait_ge(out_done[half], 16 * b + 16)
                    sp.dma_start(x_res[:, half], x_blocks[bass.ds(2 * nxt + half, 1)]
                                 .rearrange("a p t d -> p (a t) d")).then_inc(x_res_in[half], 16)
            for half in range(2):
                sp.wait_ge(x_res_in[half], 16 * (B + 1))

        @block.gpsimd
        def _(pool):
            nc.gpsimd.memset(ident[:, :], 0.0).then_inc(ident_zero, 1)
            pool.wait_ge(ident_zero, 1)
            nc.gpsimd.affine_select(out=ident[:, :], in_=ident[:, :], compare_op=ALU.not_equal, fill=1.0, base=0,
                                    pattern=[[-1, P]], channel_multiplier=1).then_inc(ident_ready, 1)
            nc.gpsimd.memset(ones, 1.0).then_inc(ones_ready, 1)
            nc.gpsimd.memset(ones_col[:, :], 1.0).then_inc(ones_ready, 1)

            def make_mask(b, t):
                k = TPG * b + t
                pool.wait_ge(adj_landed[t % 2], 16 * (MT * b + t // 2 + 1))
                pool.nop(nofuse=True)
                nc.gpsimd.tensor_scalar(masks[:, t, :], adj_in[:, t % 2, :], 1.0, 0.0, ALU.min, ALU.max)\
                    .then_inc(clamped, 1)
                pool.wait_ge(clamped, k + 1)
                pool.nop(nofuse=True)
                nc.gpsimd.tensor_scalar(masks[:, t, :], masks[:, t, :], -1.0, -NEG, ALU.add, ALU.mult)\
                    .then_inc(masks_ready, 1)

            def copy_v(b):
                pool.wait_ge(v_in, 16 * b + 16)
                pool.nop(nofuse=True)
                nc.gpsimd.tensor_copy(v_now[:, :, :], v_next[:, :, :]).then_inc(v_copied, 1)

            def sum_keys(b, p, a):
                i = 2 * (PAIRS * 2 * b + p) + a
                probs = pt[:, p % 2, a, :, :]
                pool.wait_ge(probs_ready, 2 * MT * i + 2 * MT)
                nc.gpsimd.tensor_tensor(sum4[:, :, :], probs[:, 0:4, :], probs[:, 4:8, :], ALU.add).then_inc(pair_sums, 1)
                pool.wait_ge(pair_sums, 2 * i + 1)
                nc.gpsimd.tensor_tensor(sum2[:, :, :], sum4[:, 0:2, :], sum4[:, 2:4, :], ALU.add).then_inc(pair_sums, 1)
                if later(i, 2):
                    pool.wait_ge(den_products, i // 2 if isinstance(i, int) else PAIRS * 2 * b + p)
                pool.wait_ge(pair_sums, 2 * i + 2)
                nc.gpsimd.tensor_tensor(sum1[:, a, :], sum2[:, 0, :], sum2[:, 1, :], ALU.add).then_inc(key_sums, 1)

            for k in range(2 * B):
                pool.wait_ge(h_ready, k // B + 1)
                if k >= 4:
                    pool.wait_ge(h_turned, k - 3)
                for a in range(2):
                    nc.gpsimd.tensor_copy(h_doubled[:, k % 4, :, a, :], h_rows[:, MT * k:MT * k + MT, :])\
                        .then_inc(h_doubled_ready, 1)
            for t in range(TPG):
                make_mask(0, t)
            copy_v(0)
            with pool.Fori(0, B) as b:
                for p in range(2 * PAIRS):
                    sum_keys(b, p, 0)
                    if p in (4, 5):
                        pool.wait_ge(scores_taken, UNITS * b + UNITS // 2)
                        make_mask(b + 1, 2 * (p - 4))
                        make_mask(b + 1, 2 * (p - 4) + 1)
                    sum_keys(b, p, 1)
                pool.wait_ge(scores_taken, UNITS * b + UNITS)
                for t in range(MT, TPG):
                    make_mask(b + 1, t)
                pool.wait_ge(pv_done, 2 * PAIRS * (b + 1))
                copy_v(b + 1)

        @block.tensor
        def _(pe):
            pe.wait_ge(weights_in, 16 * 9)
            pe.wait_ge(ident_ready, 1)
            for src, dst, c0 in ((wq_in, turn_banks[0], 0), (wk_in, turn_banks[0], 256), (wv_in, turn_banks[1], 0)):
                for c in range(PAIRS):
                    last = pe.transpose(dst[:, c0 + D * c:c0 + D * c + D], src[:, P * c:P * c + P], ident[0:D, 0:D])
            last.then_inc(w_turned, 1)
            pe.wait_ge(wT_ready, 3)
            pe.wait_ge(ones_ready, 1)
            pe.wait_ge(bias_products, PAIRS + 1)
            for a in range(2):
                rows = slice(D * a, D * a + D)
                first, second = score_banks[a][:, 0:512], score_banks[a][:, 512:1024]
                for c in range(PAIRS):
                    pe.matmul(first[0:D, D * c:D * c + D], wqT[rows, c, :], wkT[rows, c, :], start=True, stop=True)
                    pe.matmul(first[0:D, 256 + c:257 + c], wqT[rows, c, :], bk_col[rows, c:c + 1], start=True, stop=True)
                    pe.matmul(second[rows, D * c:D * c + D], wvT[rows, c, :], wp_in[rows, c, :], start=True, stop=True)
                    pe.matmul(second[rows, 256 + c:257 + c], wkT[rows, c, :], bq_col[rows, c:c + 1],
                              start=True, stop=True)
                sums = (o_bank, misc)[a][:, 0:PAIRS]
                pe.matmul(sums, ones[rows, :], bqk[rows, :], start=True, stop=False)
                last = pe.matmul(sums, ones[0:1, :], eb_row[:, a, :], start=False, stop=True)
            last.then_inc(fold_ready, 1)
            pe.wait_ge(wT_ready, 3)
            for c in range(PAIRS):
                pe.matmul(turn_banks[0][:, 0:D], ones, wp_bv[:, c, :], start=(c == 0), stop=False)
            pe.matmul(turn_banks[0][:, 0:D], ones[0:1, :], bp_row, start=False, stop=True).then_inc(fold_ready, 1)
            pe.wait_ge(h_ready, 2)
            pe.wait_ge(folded, 6)

            def turn_h(k):
                if k >= 4:
                    pe.wait_ge(h_lo, k - 3)
                pe.wait_ge(h_doubled_ready, 2 * k + 2)
                dst = score_banks[k % 4 // 2][:, 512 * (k % 2):512 * (k % 2) + 512]
                for t in range(MT):
                    last = pe.transpose(dst[:, P * t:P * t + P],
                                        h_doubled[:, k % 4, t].rearrange("p a d -> p (a d)"), ident[:, :])
                last.then_inc(h_turned, 1)

            def beta_block(k):
                pe.wait_ge(h_lo, k + 1)
                for t in range(MT * k, MT * k + MT):
                    dst = turn_banks[1][:, H * t:H * t + H]
                    rows = slice(P * (t % 16), P * (t % 16) + P)
                    pe.matmul(dst, h_twice_hi[:, rows], u_parts[:, :], start=True, stop=False)
                    last = pe.matmul(dst, h_twice_lo[:, rows], u_parts[:, :], start=False, stop=True)
                last.then_inc(beta_products, 1)

            for k in range(2 * B + 2):
                if k < 2 * B:
                    turn_h(k)
                if k >= 2:
                    beta_block(k - 2)
            pe.wait_ge(beta_ready, 2 * B)

            def scores(b, k):
                u = UNITS * b + k
                gb, kk = graph_of(b, k)
                p, a, mt = kk // 8, kk // MT % 2, kk % MT
                if kk == 0:
                    pe.wait_ge(parts_in, 32 * (b + k // UNITS) + 32)
                if kk % MT == 0:
                    pe.wait_ge(q_lo, 4 * PAIRS * b + k // MT + 1)
                if later(u, 2):
                    pe.wait_ge(scores_taken, u - 1)
                for j in range(2):
                    dst = score_banks[k % 2][:, 512 * j:512 * j + 512]
                    stat = qt[:, p % 2, a, P * mt:P * mt + P]
                    keys = bass.ds(M * (gb % 2) + 512 * j, 512)
                    pe.matmul(dst, stat, h_twice_hi[:, keys], start=True, stop=False)
                    last = pe.matmul(dst, stat, h_twice_lo[:, keys], start=False, stop=True)
                last.then_inc(scores_ready, 1)

            def project_q(b, k):
                gb, kk = graph_of(b, k)
                half, c = kk // (UNITS // 2), kk // 8 % PAIRS
                if kk == 0:
                    pe.wait_ge(parts_in, 32 * (b + k // UNITS) + 32)
                for i, part in enumerate((h_twice_hi, h_twice_lo)):
                    last = pe.matmul(misc[:, :], g_parts[:, P * c:P * c + P],
                                     part[:, bass.ds(M * (gb % 2) + BLK * half, BLK)], start=(i == 0), stop=(i == 1))
                last.then_inc(q_products, 1)

            def turn_y(b, k):
                u = UNITS * b + k
                pe.wait_ge(y_ready, u + 1)
                for j in range(2):
                    if later(u, 1):
                        pe.wait_ge(probs_ready, 2 * (u - 1) + j + 1)
                    for t in range(MT):
                        last = pe.transpose(turn_banks[j][:, P * t:P * t + P],
                                            w[:, k % 8, P * (MT * j + t):P * (MT * j + t) + P], ident[:, :])
                    last.then_inc(y_turned, 1)

            def step(b, k):
                pairs = 2 * PAIRS * b
                scores(b, k + 1)
                if k >= TURN:
                    turn_y(b, k - TURN)
                since = k - PV
                if since >= 0 and since % 8 < 7:
                    p, s = since // 8, since % 8
                    if s == 0:
                        pe.wait_ge(probs_ready, 16 * (pairs + p) + 16)
                        if later(pairs + p, 1):
                            pe.wait_ge(o_copied, pairs + p)
                        if p % (2 * PAIRS) == 0:
                            pe.wait_ge(v_copied, b + p // (2 * PAIRS) + 1)
                    for t in ((0, 1) if s == 0 else (s + 1,)):
                        for a in range(2):
                            last = pe.matmul(o_bank[D * a:D * a + D, :], v_now[:, t, :], pt[:, p % 2, a, t, :],
                                             start=(t == 0), stop=(t == TPG - 1))
                    if s == 6:
                        last.then_inc(pv_done, 1)
                if k >= PAIR and (k - PAIR) % 8 == 0:
                    pe.wait_ge(o_normed, pairs + (k - PAIR) // 8 + 1)
                    for t in range(MT):
                        last = pe.transpose(misc[:, P * t:P * t + P], o_norm[:, t, :], ident[:, :])
                    last.then_inc(pair_turned, 1)
                if k >= PROJECT and (k - PROJECT) % 32 == 24:
                    pe.wait_ge(pair_copied, pairs + (k - PROJECT) // 8 + 1)
                    for t in range(MT):
                        for c in range(PAIRS):
                            last = pe.matmul(misc[:, D * t:D * t + D], o_turned[:, c, P * t:P * t + P], vp[:, c, :],
                                             start=(c == 0), stop=(c == PAIRS - 1))
                    last.then_inc(out_products, 1)
                if (k + QT) % 8 == 0:
                    done = (k + QT) // 8 - 4
                    if k - PAIR >= 0:
                        pe.wait_ge(pair_copied, pairs + done + 1)
                    if k - PROJECT >= 24:
                        pe.wait_ge(out_ready, 2 * b + (k - PROJECT + 8) // 32)
                    project_q(b, k + QT)
                if k >= DEN and (k - DEN) % 8 == 0:
                    p = (k - DEN) // 8
                    pe.wait_ge(key_sums, 2 * (pairs + p) + 2)
                    pe.wait_ge(q_lo, 2 * (pairs + (k + QT) // 8) + 2)
                    for t in range(MT):
                        for a in range(2):
                            last = pe.matmul(misc[:, 2 * t + a:2 * t + a + 1], sum1[:, a, P * t:P * t + P], ones_col[:, :],
                                             start=True, stop=True)
                    last.then_inc(den_products, 1)
                if k >= ROWS and (k - ROWS) % 8 == 0:
                    p = (k - ROWS) // 8
                    pe.wait_ge(o_copied, pairs + p + 1)
                    pe.wait_ge(den_ready, pairs + p + 1)
                    for t in range(MT):
                        last = pe.transpose(misc[:, P * t:P * t + P], o_copy[:, P * t:P * t + P], ident[:, :])
                    last.then_inc(o_rows, 1)

            pe.wait_ge(parts_in, 32)
            project_q(0, 0)
            scores(0, 0)
            for k in range(K0):
                step(0, k)
            with pe.Fori(0, B) as b:
                for k in range(K0, K0 + UNITS):
                    step(b, k)

        @block.scalar
        def _(act):
            for i in range(2):
                t = slice(32 * i, 32 * i + 32)
                act.wait_ge(ln_step, 2 * i + 2)
                nc.scalar.activation(x_sq[:, t, :], x_all[:, t, :], ACT.Square).then_inc(squares_ready, 1)
            act.wait_ge(ln_step, 5)
            nc.scalar.activation(row_std, row_var, ACT.Sqrt).then_inc(std_ready, 1)
            act.wait_ge(fold_ready, 1)
            g_hi = g_parts[0:D, :].rearrange("p (c a d) -> p a c d", a=2, d=D)
            u_hi = u_parts[0:D, :].rearrange("p (c a) -> p a c", a=2)
            for a in range(2):
                nc.scalar.activation(g_hi[:, a], score_banks[a][0:D, 0:256].rearrange("p (c d) -> p c d", d=D),
                                     ACT.Copy, scale=QSCALE).then_inc(hi_weights, 1)
                nc.scalar.activation(u_hi[:, a], score_banks[a][0:D, 256:260], ACT.Copy, scale=QSCALE)\
                    .then_inc(hi_weights, 1)
            for k in range(2 * B):
                act.wait_ge(h_turned, k + 1)
                if k >= 4:
                    act.wait_ge(parts_stored[k % 4], 32 * (k // 4))
                    act.wait_ge(beta_products, k - 3)
                nc.scalar.activation(h_twice_hi[:, BLK * (k % 4):BLK * (k % 4) + BLK],
                                     score_banks[k % 4 // 2][:, 512 * (k % 2):512 * (k % 2) + 512], ACT.Copy)\
                    .then_inc(h_hi, 1)

            def q_hi_parts(b, k):
                gb, kk = graph_of(b, k)
                c = kk // 8 % PAIRS
                act.wait_ge(q_products, 2 * PAIRS * b + k // 8 + 1)
                for a in range(2):
                    rows = slice(D * a, D * a + D)
                    nc.scalar.activation(qt[0:D, kk // 8 % 2, a, :], misc[rows, :], ACT.Identity,
                                         bias=q_bias[rows, c:c + 1]).then_inc(q_hi, 1)

            def relu(b, k):
                u = UNITS * b + k
                gb, kk = graph_of(b, k)
                if later(u, 2):
                    act.wait_ge(y_ready, u - 1)
                act.wait_ge(scores_taken, u + 1)
                nc.scalar.activation(r[:, k % 2, :], w[:, k % 8, :], ACT.Relu,
                                     bias=beta[:, bass.ds(UNITS * gb + kk, 1)], scale=4.0).then_inc(relu_ready, 1)

            def exp(b, k):
                u = UNITS * b + k
                p, a, mt = k // 8, k // MT % 2, k % MT
                if k % 8 == 0 and later(2 * PAIRS * b + p, 2):
                    act.wait_ge(pv_done, 2 * PAIRS * b + p - 1)
                    act.wait_ge(key_sums, 2 * (2 * PAIRS * b + p - 1))
                for j in range(2):
                    act.wait_ge(y_turned, 2 * u + j + 1)
                    nc.scalar.activation(pt[:, p % 2, a, MT * j:MT * j + MT, P * mt:P * mt + P],
                                         turn_banks[j][:, :].rearrange("p (t m) -> p t m", t=MT),
                                         ACT.Exp, scale=0.8).then_inc(probs_ready, 1)

            def step(b, k):
                pairs = 2 * PAIRS * b
                if k >= RELU:
                    relu(b, k - RELU)
                if k >= EXP:
                    exp(b, k - EXP)
                if (k - 1 + QT) % 8 == 0:
                    q_hi_parts(b, k - 1 + QT)
                if k >= O_COPY and (k - O_COPY) % 8 == 0:
                    p = (k - O_COPY) // 8
                    act.wait_ge(pv_done, pairs + p + 1)
                    if later(pairs + p, 1):
                        act.wait_ge(o_rows, pairs + p)
                    nc.scalar.activation(o_copy[:, :], o_bank[:, :], ACT.Copy).then_inc(o_copied, 1)
                if k >= PAIR and (k - PAIR) % 8 == 0:
                    p = (k - PAIR) // 8
                    act.wait_ge(pair_turned, pairs + p + 1)
                    if p % PAIRS == 0 and later(2 * b + p // PAIRS, 1):
                        act.wait_ge(out_products, 2 * b + p // PAIRS)
                    nc.scalar.activation(o_turned[:, p % PAIRS, :], misc[:, :], ACT.Copy).then_inc(pair_copied, 1)

            act.wait_ge(folded, 6)
            q_hi_parts(0, 0)
            for k in range(K0):
                step(0, k)
            with act.Fori(0, B) as b:
                for k in range(K0, K0 + UNITS):
                    step(b, k)

        @block.vector
        def _(dve):
            for i in range(2):
                t = slice(32 * i, 32 * i + 32)
                dve.wait_ge(x_in[i], 16)
                nc.vector.tensor_reduce(row_sum[:, t], x_all[:, t, :], AX_X, ALU.add).then_inc(ln_step, 1)
                dve.wait_ge(ln_step, 2 * i + 1)
                nc.vector.scalar_tensor_tensor(x_all[:, t, :], row_sum[:, t].unsqueeze(2).to_broadcast([P, 32, D]),
                                               -1.0 / D, x_all[:, t, :], ALU.mult, ALU.add).then_inc(ln_step, 1)
            dve.wait_ge(squares_ready, 2)
            nc.vector.tensor_reduce(row_sum, x_sq, AX_X, ALU.add).then_inc(bias_products, 1)
            dve.wait_ge(weights_in, 16 * 9)
            dve.wait_ge(bias_products, 1)
            nc.vector.tensor_scalar(row_var, row_sum, 1.0 / D, EPS, ALU.mult, ALU.add).then_inc(ln_step, 1)
            nc.vector.scalar_tensor_tensor(bqk, bq_col, QSCALE, bk_col, ALU.mult, ALU.mult)
            for c in range(PAIRS):
                nc.vector.tensor_scalar(wp_bv[:, c, :], wp_in[:, c, :], bv_col[:, c:c + 1], None, ALU.mult)\
                    .then_inc(bias_products, 1)
            dve.wait_ge(w_turned, 1)
            for dst, src in ((wqT, turn_banks[0][:, 0:256]), (wkT, turn_banks[0][:, 256:512]),
                             (wvT, turn_banks[1][:, 0:256])):
                nc.vector.tensor_copy(dst, src.rearrange("p (c d) -> p c d", d=D)).then_inc(wT_ready, 1)
            dve.wait_ge(std_ready, 1)
            nc.vector.reciprocal(row_rstd, row_std).then_inc(ln_step, 1)
            dve.wait_ge(ln_step, 6)
            for i in range(2):
                t = slice(32 * i, 32 * i + 32)
                nc.vector.scalar_tensor_tensor(h_rows[:, t, :], x_all[:, t, :], 0.0,
                                               row_rstd[:, t].unsqueeze(2).to_broadcast([P, 32, D]),
                                               ALU.max, ALU.mult).then_inc(h_ready, 1)
            dve.wait_ge(fold_ready, 2)
            dve.wait_ge(hi_weights, 4)
            g_hi, g_lo = (g_parts[rows, :].rearrange("p (c a d) -> p a c d", a=2, d=D) for rows in
                          (slice(0, D), slice(D, P)))
            u_hi, u_lo = (u_parts[rows, :].rearrange("p (c a) -> p a c", a=2) for rows in (slice(0, D), slice(D, P)))
            for a in range(2):
                rows = slice(D * a, D * a + D)
                first, second = score_banks[a][:, 0:512], score_banks[a][:, 512:1024]
                nc.vector.scalar_tensor_tensor(g_lo[:, a], first[0:D, 0:256].rearrange("p (c d) -> p c d", d=D),
                                               QSCALE, g_hi[:, a].bitcast(F32), ALU.mult, ALU.subtract)
                nc.vector.scalar_tensor_tensor(u_lo[:, a], first[0:D, 256:260], QSCALE, u_hi[:, a].bitcast(F32),
                                               ALU.mult, ALU.subtract).then_inc(folded, 1)
                nc.vector.tensor_copy(vp[rows, :, :], second[rows, 0:256].rearrange("p (c d) -> p c d", d=D))
                nc.vector.tensor_scalar(q_bias[rows, :], second[rows, 256:260], QSCALE, None, ALU.mult)\
                    .then_inc(folded, 1)
                nc.vector.tensor_copy(head_const.rearrange("p (c a) -> p a c", a=2)[:, a],
                                      (o_bank, misc)[a][:, 0:PAIRS])
            nc.vector.tensor_copy(out_const[:, :], turn_banks[0][:, 0:D]).then_inc(folded, 2)
            for k in range(2 * B):
                dve.wait_ge(h_hi, k + 1)
                cols = slice(BLK * (k % 4), BLK * (k % 4) + BLK)
                nc.vector.tensor_tensor(h_twice_lo[:, cols], score_banks[k % 4 // 2][:, 512 * (k % 2):512 * (k % 2) + 512],
                                        h_twice_hi[:, cols].bitcast(F32), ALU.subtract).then_inc(h_lo, 1)
            dve.wait_ge(beta_products, 2 * B)
            for k in range(2 * B):
                last = nc.vector.tensor_tensor(beta[:, 32 * k:32 * k + 32].rearrange("p (h t) -> p h t", h=H),
                                               turn_banks[1][:, 32 * k:32 * k + 32].rearrange("p (t h) -> p h t", h=H),
                                               head_const.unsqueeze(2).to_broadcast([P, H, MT]), ALU.add)
                last.then_inc(beta_ready, 1)

            def q_lo_parts(b, k):
                gb, kk = graph_of(b, k)
                c = kk // 8 % PAIRS
                for a in range(2):
                    rows = slice(D * a, D * a + D)
                    dve.wait_ge(q_hi, 2 * (2 * PAIRS * b + k // 8) + a + 1)
                    nc.vector.scalar_tensor_tensor(qt[D:P, kk // 8 % 2, a, :], misc[rows, :], q_bias[rows, c:c + 1],
                                                   qt[0:D, kk // 8 % 2, a, :].bitcast(F32), ALU.add, ALU.subtract)\
                        .then_inc(q_lo, 1)

            def take_scores(b, k):
                u = UNITS * b + k
                gb, kk = graph_of(b, k)
                t = MT * (kk // (UNITS // 2)) + kk % MT
                if kk % (UNITS // 2) < MT:
                    dve.wait_ge(masks_ready, TPG * (b + k // UNITS) + t + 1)
                if later(u, 8):
                    dve.wait_ge(y_turned, 2 * (u - 8) + 2)
                dve.wait_ge(scores_ready, u + 1)
                dve.nop(nofuse=True)
                nc.vector.tensor_tensor_reduce(w[:, k % 8, :], score_banks[k % 2][:, :], masks[:, t, :], 0.25, LEAST,
                                               ALU.add, ALU.max, wmax[:, k // MT % 2, k % MT:k % MT + 1])\
                    .then_inc(scores_taken, 1)

            def step(b, k):
                pairs = 2 * PAIRS * b
                g = k // MT - 1
                n = UNITS // MT * b + g
                if k % MT == 0 and k >= MT:
                    gb, kk = graph_of(b, k - MT)
                    dve.wait_ge(scores_taken, MT * n + MT)
                    if later(n, 1):
                        dve.wait_ge(shift_ready, n)
                    nc.vector.scalar_tensor_tensor(shift_neg[:, :], wmax[:, g % 2, :], -5.0,
                                                   beta[:, bass.ds(UNITS * gb + kk, MT)], ALU.mult, ALU.subtract)\
                        .then_inc(neg_ready, 1)
                take_scores(b, k)
                if k % MT == 0 and k >= MT:
                    dve.wait_ge(neg_ready, n + 1)
                    nc.vector.scalar_tensor_tensor(shift[:, g % 2, :], wmax[:, g % 2, :], -1.0, shift_neg[:, :],
                                                   ALU.mult, ALU.min).then_inc(shift_ready, 1)
                if k >= Y:
                    ky = k - Y
                    dve.wait_ge(relu_ready, UNITS * b + ky + 1)
                    if ky % MT == 0:
                        dve.wait_ge(shift_ready, n + 1)
                    y = w[:, ky % 8, :]
                    nc.vector.scalar_tensor_tensor(y, y, shift[:, ky // MT % 2, ky % MT:ky % MT + 1], r[:, ky % 2, :],
                                                   ALU.add, ALU.add).then_inc(y_ready, 1)
                if (k - 1 + QT) % 8 == 0:
                    q_lo_parts(b, k - 1 + QT)
                if k >= DEN_INV and (k - DEN_INV) % 8 == 0:
                    dve.wait_ge(den_products, pairs + (k - DEN_INV) // 8 + 1)
                    nc.vector.reciprocal(den_inv[:, :], misc[:, 0:2 * MT]).then_inc(den_ready, 1)
                if k >= NORM and (k - NORM) % 8 == 0:
                    p = (k - NORM) // 8
                    dve.wait_ge(den_ready, pairs + p + 1)
                    dve.wait_ge(o_rows, pairs + p + 1)
                    nc.vector.tensor_tensor(o_norm[:, :, :].rearrange("p t (a d) -> p (t a) d", a=2),
                                            misc[:, :].rearrange("p (i d) -> p i d", d=D),
                                            den_inv[:, :].unsqueeze(2).to_broadcast([P, 2 * MT, D]), ALU.mult)\
                        .then_inc(o_normed, 1)
                if k >= FINAL - 2 and (k - FINAL + 2) % 32 == 24:
                    half = (k - FINAL + 2) // 32
                    dve.wait_ge(x_res_in[half], 16 * b + 16)
                    nc.vector.tensor_tensor(x_res[:, half], x_res[:, half],
                                            out_const[:, :].unsqueeze(1).to_broadcast([P, MT, D]), ALU.add)\
                        .then_inc(res_ready, 1)
                if k >= FINAL and (k - FINAL) % 32 == 24:
                    half = (k - FINAL) // 32
                    dve.wait_ge(res_ready, 2 * b + half + 1)
                    dve.wait_ge(out_products, 2 * b + half + 1)
                    nc.vector.tensor_tensor(out_rows[:, half], misc[:, 0:D * MT].rearrange("p (t d) -> p t d", t=MT),
                                            x_res[:, half], ALU.add).then_inc(out_ready, 1)

            q_lo_parts(0, 0)
            for k in range(K0):
                step(0, k)
            with dve.Fori(0, B) as b:
                for k in range(K0, K0 + UNITS):
                    step(b, k)


_INS = ["x", "adj", "L0_gnn_Wq", "L0_gnn_bq", "L0_gnn_Wk", "L0_gnn_bk", "L0_gnn_Wv", "L0_gnn_bv",
        "L0_gnn_edge_bias", "L0_gnn_Wp", "L0_gnn_bp"]


def kernel(**inputs):
    import numpy as _np
    import concourse.bacc as _bacc
    from concourse import mybir as _mybir
    from concourse.bass_utils import run_bass_kernel_spmd as _run

    nc = _bacc.Bacc("TRN2", target_bir_lowering=False, num_devices=1)
    arrays, args = {}, []
    for name in _INS:
        a = _np.ascontiguousarray(inputs[name])
        arrays[f"in_{name}_dram"] = a
        args.append(nc.dram_tensor(f"in_{name}_dram", a.shape, _mybir.dt.from_np(a.dtype), kind="ExternalInput").ap())
    shape = tuple(inputs["x"].shape)
    out = nc.dram_tensor("out_0_dram", shape, _mybir.dt.float32, kind="ExternalOutput").ap()
    preln_graph_attention(nc, *args, out)
    r = _run(nc, [arrays], core_ids=[0])
    return r.results[0]["out_0_dram"]
```

```python
from contextlib import ExitStack

import concourse.bass as bass
from concourse import mybir

ALU = mybir.AluOpType
ACT = mybir.ActivationFunctionType
AX_X = mybir.AxisListType.X
F32 = mybir.dt.float32
F32R = mybir.dt.float32r
BF16 = mybir.dt.bfloat16
I32 = mybir.dt.int32

P = 128
NEG = -(2.0 ** 100)
LEAST = -3.0e38
EPS = 1e-5


def preln_graph_attention(nc, x, adj, Wq, bq, Wk, bk, Wv, bv, edge_bias, Wp, bp, out):
    B, M, D = x.shape
    H = edge_bias.shape[1]
    assert (D, H, M % (8 * P)) == (64, 8, 0) and M == 1024
    TILES = B * M // P
    TPG = M // P
    MT = TPG // 2
    BLK = MT * P
    PAIRS = H // 2
    UNITS = 2 * H * MT
    QSCALE = 1.0 / 8.0
    A, Y, TURN, SUM, EXP = 3, 4, 5, 5, 6
    PV, DEN_INV, O_COPY, ROWS, NORM, ADD = 15, 18, 22, 24, 25, 26
    CONST = 22
    QT = 5
    TWO_IN = 2
    BETA = 54
    K0 = 20

    x_tiles = x.rearrange("b (t p) d -> p (b t) d", p=P)
    x_blocks = x.rearrange("b (k t p) d -> (b k) p t d", p=P, t=MT)
    out_blocks = out.rearrange("b (k t p) d -> (b k) p t d", p=P, t=MT)
    adj_tiles = adj.rearrange("b (t p) n -> (b t) p n", p=P)

    with ExitStack() as ctx:
        def sb(name, shape, dt=F32):
            return ctx.enter_context(nc.sbuf_tensor(name, shape, dt))

        def sem(name):
            return ctx.enter_context(nc.semaphore(name))

        h_twice_hi = sb("h_twice_hi", [P, 2 * M], F32R)
        h_twice_lo = sb("h_twice_lo", [P, 2 * M], F32R)
        h_stack = sb("h_stack", [P, M], F32R)
        vproj = sb("vproj", [P, TPG, PAIRS, 2 * D])
        beta = sb("beta", [P, B * UNITS])
        g_parts = sb("g_parts", [P, H * D], F32R)
        q_bias = sb("q_bias", [P, PAIRS])
        vp_hi = sb("vp_hi", [P, H * D], F32R)
        vp_lo = sb("vp_lo", [P, H * D], F32R)
        u_twice = sb("u_twice", [P, 2 * H], F32R)
        head_const = sb("head_const", [P, H])
        out_const = sb("out_const", [P, D])
        ident = sb("ident", [P, P])
        w = sb("w", [P, 8, M])
        a_line = sb("a_line", [P, 2, M])
        pt = sb("pt", [P, 2, 2, TPG, BLK])
        masks = sb("masks", [P, TPG, M], BF16)
        adj_in = sb("adj_in", [P, 2, M], I32)
        qt = sb("qt", [P, 2, 2, BLK], F32R)
        o_copy = sb("o_copy", [P, BLK])
        o_norm = sb("o_norm", [P, MT, 2 * D])
        adj_check = sb("adj_check", [P, TILES])
        check_max = sb("check_max", [P, 1])
        check_top = sb("check_top", [1, 1])
        other_kinds = sb("other_kinds", [1, 1], I32)
        minus_half = sb("minus_half", [P, 1])
        kind_bias = sb("kind_bias", [P, 5, H])
        kind_share = sb("kind_share", [P, M])
        exp_unused = sb("exp_unused", [P, M], BF16)
        x_res = sb("x_res", [P, 2, MT, D])
        wmax = sb("wmax", [P, 8])
        shift_neg = sb("shift_neg", [P, 8])
        shift = sb("shift", [P, 8])
        a_bias = sb("a_bias", [P, 8])
        den = sb("den", [P, 2, MT, 2])
        den_inv = sb("den_inv", [P, MT * 2])

        hi_store = nc.dram_tensor("hi_store", (D, B * M), F32, kind="Internal").ap()
        lo_store = nc.dram_tensor("lo_store", (D, B * M), F32, kind="Internal").ap()

        x_all = w[:, 0:4, :].rearrange("p s (t d) -> p (s t) d", d=D)
        x_sq = w[:, 4:8, :].rearrange("p s (t d) -> p (s t) d", d=D)
        temp = pt[:, :, :, :, :].rearrange("p s a t m -> p (s a t m)")
        h_doubled = temp[:, 8192:16384].rearrange("p (t a d) -> p t a d", a=2, d=D)
        wq_in, wk_in, wv_in = (temp[0:D, 512 * i:512 * i + 512] for i in range(3))
        wp_in = temp[:, 1536:1792].rearrange("p (c d) -> p c d", c=PAIRS)
        wqT, wkT, wvT = (temp[:, 2048 + 256 * i:2304 + 256 * i].rearrange("p (c d) -> p c d", c=PAIRS)
                         for i in range(3))
        bq_col, bk_col, bv_col, bqk = (temp[:, 2816 + 4 * i:2820 + 4 * i] for i in range(4))
        bp_row = temp[0:1, 2832:2896]
        eb_row = temp[0:1, 2896:2904].rearrange("p (c a) -> p a c", a=2)
        ones = temp[:, 2944:3072]
        wp_bv = temp[:, 3072:3328].rearrange("p (c d) -> p c d", c=PAIRS)
        square_sum = temp[:, 3648:3712]
        row_sum = temp[:, 3392:3456]
        row_var = temp[:, 3456:3520]
        row_std = temp[:, 3520:3584]
        row_rstd = temp[:, 3584:3648]

        bank = [ctx.enter_context(nc.psum_tensor(f"bank{i}", [P, 1024 if i < 2 else 512], F32)) for i in range(6)]
        score_banks = bank[0:2]
        turn_banks = bank[2:4]
        o_bank = bank[4]
        misc = bank[5]

        weights_in = sem("weights_in")
        x_in = [sem(f"x_in{i}") for i in range(2)]
        ident_zero = sem("ident_zero")
        ident_ready = sem("ident_ready")
        ones_ready = sem("ones_ready")
        sums_ready = sem("sums_ready")
        centered = sem("centered")
        square_sums = sem("square_sums")
        var_ready = sem("var_ready")
        rstd_ready = sem("rstd_ready")
        squares_ready = sem("squares_ready")
        std_ready = sem("std_ready")
        h_ready = sem("h_ready")
        h_twice_ready = sem("h_twice_ready")
        w_turned = sem("w_turned")
        wT_ready = sem("wT_ready")
        bias_products = sem("bias_products")
        fold_ready = sem("fold_ready")
        hi_weights = sem("hi_weights")
        folded = sem("folded")
        h_turned = sem("h_turned")
        h_hi = sem("h_hi")
        h_lo = sem("h_lo")
        parts_stored = [sem(f"parts_stored{i}") for i in range(4)]
        parts_in = sem("parts_in")
        adj_landed = [sem(f"adj_landed{i}") for i in range(2)]
        adj_checked = sem("adj_checked")
        check_ready = sem("check_ready")
        check_turned = sem("check_turned")
        kinds_known = sem("kinds_known")
        kind_steps = sem("kind_steps")
        masks_ready = sem("masks_ready")
        stack_in = sem("stack_in")
        beta_products = sem("beta_products")
        beta_parts = sem("beta_parts")
        beta_ready = sem("beta_ready")
        v_products = sem("v_products")
        v_copied = sem("v_copied")
        q_products = sem("q_products")
        q_hi = sem("q_hi")
        q_lo = sem("q_lo")
        scores_ready = sem("scores_ready")
        scores_taken = sem("scores_taken")
        neg_ready = sem("neg_ready")
        shift_ready = sem("shift_ready")
        a_bias_ready = sem("a_bias_ready")
        a_ready = sem("a_ready")
        y_ready = sem("y_ready")
        y_turned = sem("y_turned")
        probs_ready = sem("probs_ready")
        den_sums = sem("den_sums")
        den_ready = sem("den_ready")
        pv_done = sem("pv_done")
        o_copied = sem("o_copied")
        o_rows = sem("o_rows")
        o_normed = sem("o_normed")
        res_added = sem("res_added")
        x_res_in = [sem(f"x_res_in{i}") for i in range(2)]
        out_done = [sem(f"out_done{i}") for i in range(2)]

        def graph_of(b, k):
            return (b, k) if k < UNITS else (b + 1, k - UNITS)

        def runs(b, k):
            return k >= 0 and not (isinstance(b, int) and b % B == B - 1 and k >= UNITS)

        def data(b, general):
            return b - B if general else b

        def every(k, lag, period):
            return (k - lag) // period if k >= lag and (k - lag) % period == 0 else None

        def later(count, least=1):
            return not isinstance(count, int) or count >= least

        ADDS = 1 + H

        BLOCKS = [*range(2 * B - 1, 3, -1), 0, 1, 2, 3]

        def slot_before(j):
            return max(i for i in range(j) if BLOCKS[i] % 4 == BLOCKS[j] % 4)

        def added_before(b, p):
            return ADDS * (2 * b + p // PAIRS) + 1 + 2 * (p % PAIRS)

        def v_batch(b, k):
            if isinstance(b, int) and b % B == 0 and k == 1:
                return 0
            if isinstance(b, int) and b % B == 0 and k < 0:
                return None
            i = (k + 2) // 4
            if (k + 2) % 4 or i % 16 >= 8 or not runs(b, k + 2):
                return None
            return i if i < 16 else i - 8

        def beta_graph(b, k):
            if isinstance(b, int) and b % B == 0 and k == 0:
                return b
            return b + 1 if k == BETA and runs(b, UNITS) else None

        block = ctx.enter_context(nc.Block())

        @block.sync
        def _(sp):
            sp.dma_start(x_all[:, 32:64, :], x_tiles[:, 32:64, :]).then_inc(x_in[1], 16)

            def load_adj(b, n, general=False):
                if later(TPG * b + n, 2):
                    sp.wait_ge(masks_ready, TPG * b + n - 1)
                    if not general:
                        sp.wait_ge(adj_checked, TPG * b + n - 1)
                src = adj_tiles[bass.ds(TPG * data(b, general) + n, 1)].rearrange("a p n -> (a p) n")
                sp.dma_start(adj_in[:, n % 2, :], src).then_inc(adj_landed[n % 2], 16)

            def load_x(b, half, general=False):
                sp.dma_start(x_res[:, half], x_blocks[bass.ds(2 * data(b, general) + half, 1)].rearrange("a p t d -> p (a t) d"))\
                    .then_inc(x_res_in[half], 16)

            def store_out(b, half, general):
                sp.wait_ge(res_added, ADDS * (2 * b + half + 1))
                sp.dma_start(out_blocks[bass.ds(2 * data(b, general) + half, 1)].rearrange("a p t d -> p (a t) d"), x_res[:, half])\
                    .then_inc(out_done[half], 16)
                sp.wait_ge(out_done[half], 16 * b + 16)

            sp.wait_ge(x_in[0], 16)
            for n in range(2):
                load_adj(0, n)
            for j in range(2 * B):
                sp.wait_ge(h_lo, j + 1)
                k = BLOCKS[j]
                cols = slice(BLK * (k % 4), BLK * (k % 4) + BLK)
                for part, store in ((h_twice_hi, hi_store), (h_twice_lo, lo_store)):
                    sp.dma_start(store[:, BLK * k:BLK * k + BLK], part[0:D, cols].bitcast(F32))\
                        .then_inc(parts_stored[k % 4], 16)
                if j in (3, 6):
                    load_adj(0, j // 3 + 1)
            for part, rows in ((h_twice_hi, slice(0, D)), (h_twice_lo, slice(D, P))):
                sp.dma_start(h_stack[rows, :].bitcast(F32), part[rows, 0:M].bitcast(F32)).then_inc(stack_in, 16)
            for i in range(4):
                sp.wait_ge(parts_stored[i], 32 * B // 2)
            for half in range(2):
                load_x(0, half)
            for n in range(4, TPG):
                load_adj(0, n)
            def load_parts(b, general):
                rows_of = data(b, general)
                for part, store in ((h_twice_hi, hi_store), (h_twice_lo, lo_store)):
                    for rows in (slice(0, D), slice(D, P)):
                        sp.dma_start(part[rows, bass.ds(M * (b % 2), M)].bitcast(F32),
                                     store[:, bass.ds(M * rows_of, M)]).then_inc(parts_in, 16)

            def load_stack(b, general):
                rows_of = data(b, general)
                for rows, store in ((slice(0, D), hi_store), (slice(D, P), lo_store)):
                    sp.dma_start(h_stack[rows, :].bitcast(F32), store[:, bass.ds(M * rows_of, M)]).then_inc(stack_in, 16)

            def graphs(start, general):
                with sp.Fori(start, start + B - 1) as b:
                    sp.wait_ge(scores_ready, UNITS * b + 1)
                    load_parts(b + 1, general)
                    sp.wait_ge(v_products, TPG * b + TPG)
                    load_stack(b + 1, general)
                    for n in range(TPG, TPG + 4):
                        load_adj(b, n, general)
                    store_out(b, 0, general)
                    load_x(b + 1, 0, general)
                    for n in range(TPG + 4, 2 * TPG):
                        load_adj(b, n, general)
                    store_out(b, 1, general)
                    load_x(b + 1, 1, general)
                for half in range(2):
                    store_out(start + B - 1, half, general)

            graphs(0, False)
            sp.wait_ge(kinds_known, 1)
            with sp.If(sp.value_load(other_kinds[0:1, 0:1]) > 0):
                sp.wait_ge(scores_ready, UNITS * B)
                load_parts(B, True)
                sp.wait_ge(v_products, TPG * B)
                load_stack(B, True)
                for half in range(2):
                    load_x(B, half, True)
                for n in range(TPG):
                    load_adj(B, n, True)
                graphs(B, True)

        @block.gpsimd
        def _(pool):
            nc.gpsimd.memset(ident[:, :], 0.0).then_inc(ident_zero, 1)
            pool.wait_ge(ident_zero, 1)
            nc.gpsimd.affine_select(out=ident[:, :], in_=ident[:, :], compare_op=ALU.not_equal, fill=1.0, base=0,
                                    pattern=[[-1, P]], channel_multiplier=1).then_inc(ident_ready, 1)
            nc.gpsimd.memset(ones, 1.0).then_inc(ones_ready, 1)
            nc.gpsimd.memset(minus_half[:, :], -0.5).then_inc(ones_ready, 1)

            def make_mask(b, n, general):
                pool.wait_ge(adj_landed[n % 2], 16 * (MT * b + n // 2 + 1))
                g, t = n // TPG, n % TPG
                if later(b + g, 1):
                    pool.wait_ge(scores_taken, UNITS * (b + g - 1) + UNITS // 2 if t < MT else UNITS * (b + g))
                pool.nop(nofuse=True)
                first, second, *ops = (4.0, 0.0, ALU.min, ALU.max) if general else (-1.0, -NEG, ALU.add, ALU.mult)
                nc.gpsimd.tensor_scalar(masks[:, t, :], adj_in[:, n % 2, :], first, second, *ops)\
                    .then_inc(masks_ready, 1)

            def step(b, k, general):
                if runs(b, k - A):
                    u = UNITS * b + k - A
                    i = (k - A) % 8
                    if later(u, 2):
                        pool.wait_ge(y_ready, u - 1)
                    pool.wait_ge(a_bias_ready, UNITS // 2 * b + (k - A) // 2 + 1)
                    pool.nop(nofuse=True)
                    nc.gpsimd.tensor_scalar(a_line[:, i % 2, :], w[:, i, :], 5.0, a_bias[:, i:i + 1],
                                            ALU.mult, ALU.add).then_inc(a_ready, 1)
                n = (k + 28) // 8
                if k >= 4 and k % 8 == 4 and runs(b, k) and runs(b, UNITS * (n // TPG)):
                    make_mask(b, n, general)
                block_at = every(k, CONST, UNITS // 2)
                if block_at is not None and runs(b, k - CONST):
                    half = block_at % 2
                    pool.wait_ge(x_res_in[half], 16 * (b + block_at // 2) + 16)
                    nc.gpsimd.tensor_tensor(x_res[:, half], x_res[:, half],
                                            out_const[:, :].unsqueeze(1).to_broadcast([P, MT, D]), ALU.add)\
                        .then_inc(res_added, 1)
                p = every(k, ADD, 8)
                if p is not None and runs(b, k - ADD):
                    half = p // PAIRS % 2
                    pool.wait_ge(o_normed, 2 * PAIRS * b + p + 1)
                    for a in range(2):
                        pool.wait_ge(res_added, added_before(b, p) + a)
                        nc.gpsimd.tensor_tensor(x_res[:, half], x_res[:, half], o_norm[:, :, D * a:D * a + D], ALU.add)\
                            .then_inc(res_added, 1)

            def graphs(start, general):
                for n in range(4):
                    make_mask(start, n, general)
                for k in range(K0):
                    step(start, k, general)
                with pool.Fori(start, start + B - 1) as b:
                    for k in range(K0, K0 + UNITS):
                        step(b, k, general)
                for k in range(K0, K0 + UNITS):
                    step(start + B - 1, k, general)

            graphs(0, False)
            pool.wait_ge(kinds_known, 1)
            with pool.If(pool.value_load(other_kinds[0:1, 0:1]) > 0):
                graphs(B, True)

        @block.tensor
        def _(pe):
            pe.wait_ge(weights_in, 16 * 10)
            pe.wait_ge(ident_ready, 1)
            for src, dst, c0 in ((wq_in, turn_banks[0], 0), (wk_in, turn_banks[0], 256), (wv_in, turn_banks[1], 0)):
                for c in range(PAIRS):
                    last = pe.transpose(dst[:, c0 + D * c:c0 + D * c + D], src[:, P * c:P * c + P], ident[0:D, 0:D])
            last.then_inc(w_turned, 1)
            pe.wait_ge(wT_ready, 3)
            pe.wait_ge(ones_ready, 1)
            pe.wait_ge(bias_products, PAIRS)
            for a in range(2):
                rows = slice(D * a, D * a + D)
                first, second = score_banks[a][:, 0:512], score_banks[a][:, 512:1024]
                for c in range(PAIRS):
                    pe.matmul(first[0:D, D * c:D * c + D], wqT[rows, c, :], wkT[rows, c, :], start=True, stop=True)
                    pe.matmul(first[0:D, 256 + c:257 + c], wqT[rows, c, :], bk_col[rows, c:c + 1], start=True, stop=True)
                    pe.matmul(second[0:D, D * c:D * c + D], wvT[rows, c, :], wp_in[rows, c, :], start=True, stop=True)
                    pe.matmul(second[rows, 256 + c:257 + c], wkT[rows, c, :], bq_col[rows, c:c + 1],
                              start=True, stop=True)
                sums = (o_bank, misc)[a][:, 0:PAIRS]
                pe.matmul(sums, ones[rows, :], bqk[rows, :], start=True, stop=False)
                last = pe.matmul(sums, ones[0:1, :], eb_row[:, a, :], start=False, stop=True)
            last.then_inc(fold_ready, 1)
            for c in range(PAIRS):
                pe.matmul(turn_banks[0][:, 0:D], ones, wp_bv[:, c, :], start=(c == 0), stop=False)
            pe.matmul(turn_banks[0][:, 0:D], ones[0:1, :], bp_row, start=False, stop=True).then_inc(fold_ready, 1)
            pe.wait_ge(folded, 6)

            def turn_h(j):
                k = BLOCKS[j]
                pe.wait_ge(h_twice_ready, 1 + (k < B))
                if j >= 4:
                    pe.wait_ge(h_lo, slot_before(j) + 1)
                dst = score_banks[k % 4 // 2][:, 512 * (k % 2):512 * (k % 2) + 512]
                for t in range(MT):
                    last = pe.transpose(dst[:, P * t:P * t + P],
                                        h_doubled[:, MT * k + t].rearrange("p a d -> p (a d)"), ident[:, :])
                last.then_inc(h_turned, 1)

            for j in range(2 * B):
                turn_h(j)

            def scores(b, k):
                u = UNITS * b + k
                gb, kk = graph_of(b, k)
                p, a, mt = kk // 8, kk // MT % 2, kk % MT
                if kk % MT == 0:
                    pe.wait_ge(q_lo, 4 * PAIRS * b + k // MT + 1)
                if later(u, 2):
                    pe.wait_ge(scores_taken, u - 1)
                for j in range(2):
                    dst = score_banks[k % 2][:, 512 * j:512 * j + 512]
                    stat = qt[:, p % 2, a, P * mt:P * mt + P]
                    keys = bass.ds(M * (gb % 2) + 512 * j, 512)
                    pe.matmul(dst, stat, h_twice_hi[:, keys], start=True, stop=False)
                    last = pe.matmul(dst, stat, h_twice_lo[:, keys], start=False, stop=True)
                last.then_inc(scores_ready, 1)

            def free_misc(b, k):
                for past in range(k - 1, k - 24, -1):
                    if every(past, ROWS, 8) is not None and runs(b, past - ROWS):
                        return pe.wait_ge(o_normed, 2 * PAIRS * b + every(past, ROWS, 8) + 1)
                    if isinstance(b, int) and (b, past) == (B - 1, BETA):
                        return pe.wait_ge(check_ready, 2)
                    if beta_graph(b, past) is not None:
                        return pe.wait_ge(beta_ready, 2 * beta_graph(b, past) + 2)
                    if v_batch(b, past) is not None:
                        return pe.wait_ge(v_copied, TPG * b + v_batch(b, past) + 1)
                    if (past + QT) % 8 == 0 and runs(b, past + QT):
                        return pe.wait_ge(q_lo, 2 * (2 * PAIRS * b + (past + QT) // 8) + 2)

            def project_q(b, k):
                gb, kk = graph_of(b, k)
                half, c = kk // (UNITS // 2), kk // 8 % PAIRS
                if k == UNITS:
                    pe.wait_ge(parts_in, 64 * b + 64)
                for i, part in enumerate((h_twice_hi, h_twice_lo)):
                    last = pe.matmul(misc[:, :], g_parts[:, P * c:P * c + P],
                                     part[:, bass.ds(M * (gb % 2) + BLK * half, BLK)], start=(i == 0), stop=(i == 1))
                last.then_inc(q_products, 1)

            def project_v(b, i):
                heads = slice(256 * (i % TPG // 4), 256 * (i % TPG // 4) + 256)
                if i % TPG == 0:
                    pe.wait_ge(stack_in, 32 * (b + i // TPG) + 32)
                for j in range(2):
                    dst = misc[:, 256 * j:256 * j + 256]
                    keys = slice(P * (i % 4 * 2 + j), P * (i % 4 * 2 + j) + P)
                    pe.matmul(dst, h_stack[:, keys], vp_hi[:, heads], start=True, stop=False)
                    last = pe.matmul(dst, h_stack[:, keys], vp_lo[:, heads], start=False, stop=True)
                last.then_inc(v_products, 1)

            def project_beta(g):
                pe.wait_ge(stack_in, 32 * g + 32)
                for t in range(TPG):
                    last = pe.matmul(misc[:, 2 * H * t:2 * H * t + 2 * H], h_stack[:, P * t:P * t + P], u_twice[:, :],
                                     start=True, stop=True)
                last.then_inc(beta_products, 1)

            def turn_y(b, k):
                u = UNITS * b + k
                pe.wait_ge(y_ready, u + 1)
                for j in range(2):
                    if later(u, 1):
                        pe.wait_ge(probs_ready, 2 * (u - 1) + j + 1)
                    for t in range(MT):
                        last = pe.transpose(turn_banks[j][:, P * t:P * t + P],
                                            w[:, k % 8, P * (MT * j + t):P * (MT * j + t) + P], ident[:, :])
                    last.then_inc(y_turned, 1)

            def weigh_v(b, p, s):
                if s == 0:
                    pe.wait_ge(probs_ready, 16 * (2 * PAIRS * b + p) + 16)
                    if later(2 * PAIRS * b + p, 1):
                        pe.wait_ge(o_copied, 2 * PAIRS * b + p)
                    if p % (2 * PAIRS) < PAIRS:
                        pe.wait_ge(v_copied, TPG * (b + p // (2 * PAIRS)) + 4 * (p % PAIRS // 2) + 4)
                for t in range(s if s <= TWO_IN else s + 1, s + 1 if s < TWO_IN else s + 2):
                    for a in range(2):
                        last = pe.matmul(o_bank[D * a:D * a + D, :], vproj[:, t, p % PAIRS, D * a:D * a + D],
                                         pt[:, p % 2, a, t, :], start=(t == 0), stop=(t == TPG - 1))
                if s == TPG - 2:
                    last.then_inc(pv_done, 1)

            def step(b, k):
                if runs(b, k + 1):
                    scores(b, k + 1)
                i = v_batch(b, k)
                if i is not None:
                    free_misc(b, k)
                    project_v(b, i)
                g = beta_graph(b, k)
                if g is not None:
                    free_misc(b, k)
                    project_beta(g)
                if isinstance(b, int) and (b, k) == (B - 1, BETA):
                    free_misc(b, k)
                    pe.wait_ge(check_ready, 1)
                    pe.transpose(misc[0:1, 0:P], check_max[:, :], ident[:, :]).then_inc(check_turned, 1)
                if (k + QT) % 8 == 0 and runs(b, k + QT):
                    free_misc(b, k)
                    project_q(b, k + QT)
                if k >= PV and (k - PV) % 8 < TPG - 1 and runs(b, k - PV):
                    weigh_v(b, (k - PV) // 8, (k - PV) % 8)
                p = every(k, ROWS, 8)
                if p is not None and runs(b, k - ROWS):
                    free_misc(b, k)
                    pe.wait_ge(o_copied, 2 * PAIRS * b + p + 1)
                    for t in range(MT):
                        last = pe.transpose(misc[:, P * t:P * t + P], o_copy[:, P * t:P * t + P], ident[:, :])
                    last.then_inc(o_rows, 1)
                if runs(b, k - TURN):
                    turn_y(b, k - TURN)

            pe.wait_ge(h_lo, 2 * B - 2)
            def graphs(start):
                project_q(start, 0)
                scores(start, 0)
                for k in range(K0):
                    step(start, k)
                with pe.Fori(start, start + B - 1) as b:
                    for k in range(K0, K0 + UNITS):
                        step(b, k)
                for k in range(K0, K0 + UNITS):
                    step(start + B - 1, k)

            graphs(0)
            pe.wait_ge(kinds_known, 1)
            with pe.If(pe.value_load(other_kinds[0:1, 0:1]) > 0):
                pe.wait_ge(parts_in, 64 * B)
                pe.wait_ge(o_normed, 2 * PAIRS * B)
                graphs(B)

        @block.scalar
        def _(act):
            for dst, src in ((wq_in, Wq), (wk_in, Wk), (wv_in, Wv),
                             (wp_in, Wp.rearrange("(c p) d -> p c d", p=P))):
                act.dma_start(dst, src).then_inc(weights_in, 16)
            for dst, src in ((bq_col, bq), (bk_col, bk), (bv_col, bv)):
                with nc.allow_non_contiguous_dma(reason="three vectors of 512"):
                    act.dma_start(dst, src.rearrange("(c p) -> p c", p=P)).then_inc(weights_in, 16)
            act.dma_start(bp_row, bp.rearrange("(a d) -> a d", a=1)).then_inc(weights_in, 16)
            act.dma_start(temp[0:1, 2896:2904], edge_bias[1:2, :]).then_inc(weights_in, 16)
            act.dma_start(kind_bias[:, :, :].rearrange("p k h -> p (k h)"),
                          edge_bias.rearrange("(a k) h -> a (k h)", a=1).to_broadcast([P, 5 * H])).then_inc(weights_in, 16)
            act.dma_start(x_all[:, 0:32, :], x_tiles[:, 0:32, :]).then_inc(x_in[0], 16)

            def check_adj(b, n):
                i = TPG * b + n
                act.wait_ge(adj_landed[n % 2], 16 * (MT * b + n // 2 + 1))
                if later(i, 1):
                    act.wait_ge(adj_checked, i)
                nc.scalar.activation(exp_unused[:, :], adj_in[:, n % 2, :], ACT.Square, bias=minus_half[:, :],
                                     accum_out=adj_check[:, bass.ds(i, 1)]).then_inc(adj_checked, 1)

            for i in (1, 0):
                t = slice(32 * i, 32 * i + 32)
                act.wait_ge(centered, 2 - i)
                nc.scalar.activation(x_sq[:, t, :], x_all[:, t, :], ACT.Square).then_inc(squares_ready, 1)
                if i == 1:
                    act.wait_ge(w_turned, 1)
                    for dst, src in ((wqT, turn_banks[0][:, 0:256]), (wkT, turn_banks[0][:, 256:512]),
                                     (wvT, turn_banks[1][:, 0:256])):
                        nc.scalar.activation(dst, src.rearrange("p (c d) -> p c d", d=D), ACT.Copy)\
                            .then_inc(wT_ready, 1)
            for i in (1, 0):
                t = slice(32 * i, 32 * i + 32)
                act.wait_ge(var_ready, 2 - i)
                nc.scalar.activation(row_std[:, t], row_var[:, t], ACT.Sqrt).then_inc(std_ready, 1)
            act.wait_ge(ones_ready, 2)
            for n in range(2):
                check_adj(0, n)
            act.wait_ge(fold_ready, 1)
            g_hi = g_parts[0:D, :].rearrange("p (c a d) -> p a c d", a=2, d=D)
            for a in range(2):
                first, second = score_banks[a][:, 0:512], score_banks[a][:, 512:1024]
                nc.scalar.activation(g_hi[:, a], first[0:D, 0:256].rearrange("p (c d) -> p c d", d=D),
                                     ACT.Copy, scale=QSCALE).then_inc(hi_weights, 1)
                for rows in (slice(0, D), slice(D, P)):
                    nc.scalar.activation(u_twice[rows, 0:H].rearrange("p (c a) -> p a c", a=2)[:, a],
                                         first[0:D, 256:260], ACT.Copy, scale=QSCALE).then_inc(hi_weights, 1)
                    nc.scalar.activation(vp_hi[rows, :].rearrange("p (c a d) -> p a c d", a=2, d=D)[:, a],
                                         second[0:D, 0:256].rearrange("p (c d) -> p c d", d=D), ACT.Copy)\
                        .then_inc(hi_weights, 1)
            for n, i in enumerate((1, 0)):
                act.wait_ge(h_ready, n + 1)
                t = slice(32 * i, 32 * i + 32)
                nc.scalar.activation(h_doubled[:, t, 1, :], h_doubled[:, t, 0, :], ACT.Copy).then_inc(h_twice_ready, 1)
            for j in range(2 * B):
                k = BLOCKS[j]
                act.wait_ge(h_turned, j + 1)
                if j >= 4:
                    act.wait_ge(parts_stored[k % 4], 32 * (j // 4))
                nc.scalar.activation(h_twice_hi[:, BLK * (k % 4):BLK * (k % 4) + BLK],
                                     score_banks[k % 4 // 2][:, 512 * (k % 2):512 * (k % 2) + 512], ACT.Copy)\
                    .then_inc(h_hi, 1)

            def q_hi_parts(b, k):
                c = k // 8 % PAIRS
                act.wait_ge(q_products, 2 * PAIRS * b + k // 8 + 1)
                for a in range(2):
                    rows = slice(D * a, D * a + D)
                    nc.scalar.activation(qt[0:D, k // 8 % 2, a, :], misc[rows, :], ACT.Identity,
                                         bias=q_bias[rows, c:c + 1]).then_inc(q_hi, 1)

            def copy_v(b, i):
                c, t = i % TPG // 4 * 2, i % 4 * 2
                act.wait_ge(v_products, TPG * b + i + 1)
                if later(TPG * b + i, TPG):
                    act.wait_ge(pv_done, 2 * PAIRS * (b + i // TPG - 1) + PAIRS + c + 2)
                nc.scalar.activation(vproj[:, t:t + 2, c:c + 2, :],
                                     misc[:, :].rearrange("p (t c d) -> p t c d", t=2, c=2), ACT.Copy)\
                    .then_inc(v_copied, 1)

            def exp(b, k):
                u = UNITS * b + k
                p, a, mt = k // 8, k // MT % 2, k % MT
                if k % 8 == 0 and later(2 * PAIRS * b + p, 2):
                    act.wait_ge(pv_done, 2 * PAIRS * b + p - 1)
                for j in range(2):
                    act.wait_ge(y_turned, 2 * u + j + 1)
                    nc.scalar.activation(pt[:, p % 2, a, MT * j:MT * j + MT, P * mt:P * mt + P],
                                         turn_banks[j][:, :].rearrange("p (t m) -> p t m", t=MT),
                                         ACT.Exp, scale=0.8).then_inc(probs_ready, 1)

            def sum_exp(b, k, general):
                u = UNITS * b + k
                p, a, mt = k // 8, k // MT % 2, k % MT
                if k % 8 == 0 and later(2 * PAIRS * b + p, 2):
                    act.wait_ge(den_ready, 2 * PAIRS * b + p - 1)
                if later(u, 1):
                    act.wait_ge(den_sums, u)
                if not general:
                    checks = 4 + (k + SUM - 2) // 8
                    act.wait_ge(adj_checked, TPG * b + (checks if runs(b, UNITS) else min(checks, TPG)))
                act.wait_ge(y_ready, u + 1)
                nc.scalar.activation(exp_unused[:, :], w[:, k % 8, :], ACT.Exp, scale=0.8,
                                     accum_out=den[:, p % 2, mt, a:a + 1]).then_inc(den_sums, 1)

            def step(b, k, general):
                if runs(b, k - EXP):
                    exp(b, k - EXP)
                if (k + QT) % 8 == 0 and runs(b, k + QT):
                    q_hi_parts(b, k + QT)
                i = v_batch(b, k)
                if i is not None:
                    copy_v(b, i)
                if runs(b, k - SUM):
                    sum_exp(b, k - SUM, general)
                n = (k + 23) // 8
                if not general and k >= 9 and k % 8 == 1 and runs(b, UNITS * (n // TPG)):
                    act.wait_ge(den_sums, UNITS * b + k - SUM + 1)
                    check_adj(b, n)

            act.wait_ge(folded, 6)
            def graphs(start, general):
                q_hi_parts(start, 0)
                if not general:
                    for n in (2, 3):
                        check_adj(start, n)
                for k in range(K0):
                    step(start, k, general)
                with act.Fori(start, start + B - 1) as b:
                    for k in range(K0, K0 + UNITS):
                        step(b, k, general)
                for k in range(K0, K0 + UNITS):
                    step(start + B - 1, k, general)

            graphs(0, False)
            act.wait_ge(kinds_known, 1)
            with act.If(act.value_load(other_kinds[0:1, 0:1]) > 0):
                graphs(B, True)

        @block.vector
        def _(dve):
            halves = {i: slice(32 * i, 32 * i + 32) for i in (1, 0)}

            def center(i):
                t = halves[i]
                dve.wait_ge(x_in[i], 16)
                nc.vector.tensor_reduce(row_sum[:, t], x_all[:, t, :], AX_X, ALU.add).then_inc(sums_ready, 1)
                dve.wait_ge(sums_ready, 2 - i)
                nc.vector.scalar_tensor_tensor(x_all[:, t, :], row_sum[:, t].unsqueeze(2).to_broadcast([P, 32, D]),
                                               -1.0 / D, x_all[:, t, :], ALU.mult, ALU.add).then_inc(centered, 1)

            center(1)
            dve.wait_ge(weights_in, 16 * 10)
            for kind in range(2, 5):
                nc.vector.tensor_tensor(kind_bias[:, kind, :], kind_bias[:, kind, :], kind_bias[:, 1, :], ALU.subtract)
            nc.vector.scalar_tensor_tensor(bqk, bq_col, QSCALE, bk_col, ALU.mult, ALU.mult)
            for c in range(PAIRS):
                nc.vector.tensor_scalar(wp_bv[:, c, :], wp_in[:, c, :], bv_col[:, c:c + 1], None, ALU.mult)\
                    .then_inc(bias_products, 1)
            center(0)
            for i, t in halves.items():
                dve.wait_ge(squares_ready, 2 - i)
                nc.vector.tensor_reduce(square_sum[:, t], x_sq[:, t, :], AX_X, ALU.add).then_inc(square_sums, 1)
                dve.wait_ge(square_sums, 2 - i)
                nc.vector.tensor_scalar(row_var[:, t], square_sum[:, t], 1.0 / D, EPS, ALU.mult, ALU.add)\
                    .then_inc(var_ready, 1)
            def lo_weights():
                dve.wait_ge(fold_ready, 2)
                dve.wait_ge(hi_weights, 10)
                both = slice(0, D), slice(D, P)
                for a in range(2):
                    first, second = score_banks[a][:, 0:512], score_banks[a][:, 512:1024]
                    g_hi, g_lo = (g_parts[rows, :].rearrange("p (c a d) -> p a c d", a=2, d=D)[:, a] for rows in both)
                    nc.vector.scalar_tensor_tensor(g_lo, first[0:D, 0:256].rearrange("p (c d) -> p c d", d=D),
                                                   QSCALE, g_hi.bitcast(F32), ALU.mult, ALU.subtract)
                    for rows in both:
                        hi, lo = (part[rows, :].rearrange("p (c a d) -> p a c d", a=2, d=D)[:, a]
                                  for part in (vp_hi, vp_lo))
                        nc.vector.tensor_tensor(lo, second[0:D, 0:256].rearrange("p (c d) -> p c d", d=D),
                                                hi.bitcast(F32), ALU.subtract)
                        hi, lo = (u_twice[rows, H * i:H * i + H].rearrange("p (c a) -> p a c", a=2)[:, a]
                                  for i in range(2))
                        nc.vector.scalar_tensor_tensor(lo, first[0:D, 256:260], QSCALE, hi.bitcast(F32),
                                                       ALU.mult, ALU.subtract).then_inc(folded, 1)
                    rows = both[a]
                    nc.vector.tensor_scalar(q_bias[rows, :], second[rows, 256:260], QSCALE, None, ALU.mult)
                    nc.vector.tensor_copy(head_const[:, :].rearrange("p (c a) -> p a c", a=2)[:, a],
                                          (o_bank, misc)[a][:, 0:PAIRS])
                nc.vector.tensor_copy(out_const[:, :], turn_banks[0][:, 0:D]).then_inc(folded, 2)

            for i, t in halves.items():
                dve.wait_ge(std_ready, 2 - i)
                nc.vector.reciprocal(row_rstd[:, t], row_std[:, t]).then_inc(rstd_ready, 1)
                dve.wait_ge(rstd_ready, 2 - i)
                nc.vector.scalar_tensor_tensor(h_doubled[:, t, 0, :], x_all[:, t, :], 0.0,
                                               row_rstd[:, t].unsqueeze(2).to_broadcast([P, 32, D]),
                                               ALU.max, ALU.mult).then_inc(h_ready, 1)
                if i == 1:
                    lo_weights()
            for j in range(2 * B):
                k = BLOCKS[j]
                dve.wait_ge(h_hi, j + 1)
                cols = slice(BLK * (k % 4), BLK * (k % 4) + BLK)
                nc.vector.tensor_tensor(h_twice_lo[:, cols], score_banks[k % 4 // 2][:, 512 * (k % 2):512 * (k % 2) + 512],
                                        h_twice_hi[:, cols].bitcast(F32), ALU.subtract).then_inc(h_lo, 1)

            def add_beta(g, general):
                parts = misc[:, 0:2 * H * TPG].rearrange("p (t i h) -> p i h t", i=2, h=H)
                dve.wait_ge(beta_products, g + 1)
                consts = head_const[:, :].unsqueeze(2).to_broadcast([P, H, MT])
                for half in range(2):
                    dst = beta[:, bass.ds(UNITS * data(g, general) + UNITS // 2 * half, UNITS // 2)].rearrange("p (h t) -> p h t", h=H)
                    t = slice(MT * half, MT * half + MT)
                    nc.vector.tensor_tensor(dst, parts[:, 0, :, t], consts, ALU.add).then_inc(beta_parts, 1)
                    dve.wait_ge(beta_parts, 2 * g + half + 1)
                    nc.vector.tensor_tensor(dst, parts[:, 1, :, t], dst, ALU.add).then_inc(beta_ready, 1)

            def q_lo_part(b, k, a):
                c = k // 8 % PAIRS
                rows = slice(D * a, D * a + D)
                dve.wait_ge(q_hi, 2 * (2 * PAIRS * b + k // 8) + a + 1)
                nc.vector.scalar_tensor_tensor(qt[D:P, k // 8 % 2, a, :], misc[rows, :], q_bias[rows, c:c + 1],
                                               qt[0:D, k // 8 % 2, a, :].bitcast(F32), ALU.add, ALU.subtract)\
                    .then_inc(q_lo, 1)

            def kind_biases(b, k, t):
                head, share, unit_bias = k // MT % H, kind_share[:, :], w[:, k % 8, :]
                n = 7 * (UNITS * b + k) - 7 * UNITS * B
                nc.vector.tensor_scalar(unit_bias, masks[:, t, :], 0.0, NEG, ALU.is_equal, ALU.mult)\
                    .then_inc(kind_steps, 1)
                for i, kind in enumerate((2, 3, 4)):
                    if later(n + 2 * i, 1):
                        dve.wait_ge(kind_steps, n + 2 * i + 1 if i else n)
                    nc.vector.tensor_scalar(share, masks[:, t, :], float(kind), kind_bias[:, kind, head:head + 1],
                                            ALU.is_equal, ALU.mult).then_inc(kind_steps, 1)
                    dve.wait_ge(kind_steps, n + 2 * i + 2)
                    nc.vector.tensor_tensor(unit_bias, unit_bias, share, ALU.add).then_inc(kind_steps, 1)
                dve.wait_ge(kind_steps, n + 7)

            def take_scores(b, k, general):
                u = UNITS * b + k
                t = MT * (k // (UNITS // 2)) % TPG + k % MT
                if k % (UNITS // 2) < MT:
                    dve.wait_ge(masks_ready, TPG * (b + k // UNITS) + t + 1)
                if later(u, 8):
                    dve.wait_ge(y_turned, 2 * (u - 8) + 2)
                    dve.wait_ge(den_sums, u - 7)
                dve.wait_ge(scores_ready, u + 1)
                if general:
                    kind_biases(b, k, t)
                dve.nop(nofuse=True)
                nc.vector.tensor_tensor_reduce(w[:, k % 8, :], score_banks[k % 2][:, :],
                                               w[:, k % 8, :] if general else masks[:, t, :], 0.25, LEAST,
                                               ALU.add, ALU.max, wmax[:, k % 8:k % 8 + 1]).then_inc(scores_taken, 1)

            def step(b, k, general):
                two = k % 2 == 0 and runs(b, k - 2)
                n = UNITS // 2 * b + k // 2 - 1
                cols = slice((k - 2) % 8, (k - 2) % 8 + 2)
                beta_two = beta[:, bass.ds(UNITS * data(b, general) + k - 2, 2)] if two else None
                if two:
                    if k % UNITS == 2:
                        dve.wait_ge(beta_ready, 2 * (b + k // UNITS) + 2)
                    dve.wait_ge(scores_taken, UNITS * b + k)
                    nc.vector.scalar_tensor_tensor(shift_neg[:, cols], wmax[:, cols], -5.0, beta_two,
                                                   ALU.mult, ALU.subtract).then_inc(neg_ready, 1)
                if runs(b, k):
                    take_scores(b, k, general)
                if two:
                    dve.wait_ge(neg_ready, n + 1)
                    nc.vector.scalar_tensor_tensor(shift[:, cols], wmax[:, cols], -1.0, shift_neg[:, cols],
                                                   ALU.mult, ALU.min).then_inc(shift_ready, 1)
                if runs(b, k - Y):
                    i = (k - Y) % 8
                    dve.wait_ge(a_ready, UNITS * b + k - Y + 1)
                    nc.vector.scalar_tensor_tensor(w[:, i, :], w[:, i, :], shift[:, i:i + 1], a_line[:, i % 2, :],
                                                   ALU.add, ALU.max).then_inc(y_ready, 1)
                p = every(k, O_COPY, 8)
                if p is not None and runs(b, k - O_COPY):
                    dve.wait_ge(pv_done, 2 * PAIRS * b + p + 1)
                    if later(2 * PAIRS * b + p, 1):
                        dve.wait_ge(o_rows, 2 * PAIRS * b + p)
                    nc.vector.tensor_copy(o_copy[:, :], o_bank[:, :]).then_inc(o_copied, 1)
                if two:
                    dve.wait_ge(shift_ready, n + 1)
                    nc.vector.tensor_tensor(a_bias[:, cols], shift[:, cols], beta_two, ALU.add)\
                        .then_inc(a_bias_ready, 1)
                for a in range(2):
                    first = k - 1 - a + QT
                    if first % 8 == 0 and first >= 8 and runs(b, first):
                        q_lo_part(b, first, a)
                g = beta_graph(b, k - 1)
                if g is not None:
                    add_beta(g, general)
                if isinstance(b, int) and b == B - 1:
                    if k == 40:
                        dve.wait_ge(adj_checked, TILES)
                        nc.vector.tensor_reduce(check_max[:, :], adj_check[:, :], AX_X, ALU.max).then_inc(check_ready, 1)
                    if k == BETA + 1:
                        dve.wait_ge(check_turned, 1)
                        nc.vector.tensor_reduce(check_top[:, :], misc[0:1, 0:P], AX_X, ALU.max).then_inc(check_ready, 1)
                        dve.wait_ge(check_ready, 2)
                        nc.vector.tensor_scalar(other_kinds[:, :], check_top[:, :], M / 4.0, None, ALU.is_gt)\
                            .then_inc(kinds_known, 1)
                p = every(k, DEN_INV, 8)
                if p is not None and runs(b, k - DEN_INV):
                    dve.wait_ge(den_sums, 8 * (2 * PAIRS * b + p) + 8)
                    if later(2 * PAIRS * b + p, 1):
                        dve.wait_ge(o_normed, 2 * PAIRS * b + p)
                    nc.vector.reciprocal(den_inv[:, :], den[:, p % 2].rearrange("p t a -> p (t a)"))\
                        .then_inc(den_ready, 1)
                p = every(k, NORM, 8)
                if p is not None and runs(b, k - NORM):
                    dve.wait_ge(o_rows, 2 * PAIRS * b + p + 1)
                    dve.wait_ge(den_ready, 2 * PAIRS * b + p + 1)
                    if later(2 * PAIRS * b + p, 1):
                        dve.wait_ge(res_added, added_before(b, p - 1) + 2)
                    nc.vector.tensor_tensor(o_norm[:, :, :].rearrange("p t (a d) -> p (t a) d", a=2),
                                            misc[:, :].rearrange("p (i d) -> p i d", d=D),
                                            den_inv[:, :].unsqueeze(2).to_broadcast([P, 2 * MT, D]), ALU.mult)\
                        .then_inc(o_normed, 1)

            def graphs(start, general):
                for a in range(2):
                    q_lo_part(start, 0, a)
                for k in range(K0):
                    step(start, k, general)
                with dve.Fori(start, start + B - 1) as b:
                    for k in range(K0, K0 + UNITS):
                        step(b, k, general)
                for k in range(K0, K0 + UNITS):
                    step(start + B - 1, k, general)

            graphs(0, False)
            dve.wait_ge(kinds_known, 1)
            with dve.If(dve.value_load(other_kinds[0:1, 0:1]) > 0):
                graphs(B, True)


_INS = ["x", "adj", "L0_gnn_Wq", "L0_gnn_bq", "L0_gnn_Wk", "L0_gnn_bk", "L0_gnn_Wv", "L0_gnn_bv",
        "L0_gnn_edge_bias", "L0_gnn_Wp", "L0_gnn_bp"]


def kernel(**inputs):
    import numpy as _np
    import concourse.bacc as _bacc
    from concourse import mybir as _mybir
    from concourse.bass_utils import run_bass_kernel_spmd as _run

    nc = _bacc.Bacc("TRN2", target_bir_lowering=False, num_devices=1)
    arrays, args = {}, []
    for name in _INS:
        a = _np.ascontiguousarray(inputs[name])
        arrays[f"in_{name}_dram"] = a
        args.append(nc.dram_tensor(f"in_{name}_dram", a.shape, _mybir.dt.from_np(a.dtype), kind="ExternalInput").ap())
    shape = tuple(inputs["x"].shape)
    out = nc.dram_tensor("out_0_dram", shape, _mybir.dt.float32, kind="ExternalOutput").ap()
    preln_graph_attention(nc, *args, out)
    r = _run(nc, [arrays], core_ids=[0])
    return r.results[0]["out_0_dram"]
```
